# Optimizing a Trainium2 kernel written in Bass

```python
import numpy as np
import jax
import jax.numpy as jnp

def _softmax(x, axis=-1):
    return jax.nn.softmax(x, axis=axis)

def _gelu(x):
    return jax.nn.gelu(x, approximate=True)

def _silu(x):
    return jax.nn.silu(x)

def _sigmoid(x):
    return jax.nn.sigmoid(x)

def _layernorm(x, axis=-1, eps=1e-05):
    m = jnp.mean(x, axis=axis, keepdims=True)
    v = jnp.var(x, axis=axis, keepdims=True)
    return (x - m) / jnp.sqrt(v + eps)

def _scatter_add(tgt, idx, src, axis=0):
    return tgt.at[idx].add(src)

def _segment_sum(src, seg, n):
    return jax.ops.segment_sum(src, seg, n)
kernel_name = 'mk_decoder_postln_d1_seqx_r4_3d5645'

def setup_inputs(seed: int=0):
    np.random.seed(seed)
    _w = jnp.asarray

    def _rec_inputs():
        import jax
        import jax.numpy as jnp
        _rk = jax.random.key(seed)
        x = -0.0003929 + 0.9999 * jax.random.normal(jax.random.fold_in(_rk, 1), (8, 512, 256), jnp.float32)
        _lenS = 512 - jax.random.randint(jax.random.fold_in(_rk, 7), (8,), 0, max(1, 512 // 4) + 1, jnp.int32)
        _lenS2 = 512 - jax.random.randint(jax.random.fold_in(_rk, 8), (8,), 0, max(1, 512 // 4) + 1, jnp.int32)
        _ctx_768P = jax.random.normal(jax.random.fold_in(_rk, 11), (8, 16, 192), jnp.float32)
        _ctx_768c = jax.random.dirichlet(jax.random.fold_in(_rk, 511), 0.3 * jnp.ones((16,), jnp.float32), (8, 512))
        _ctx_768t = jnp.einsum('bsk,bkd->bsd', _ctx_768c, _ctx_768P)
        _ctx_768t = _ctx_768t * jax.lax.rsqrt(jnp.mean(jnp.square(_ctx_768t)) + 1e-12) * 0.953939
        ctx_768 = 2.09791e-05 + 1.00001 * (_ctx_768t + 0.3 * jax.random.normal(jax.random.fold_in(_rk, 611), (8, 512, 192), jnp.float32))
        return (x, ctx_768)
    x, ctx_768 = _rec_inputs()

    def _L0_attn_setup():
        import jax, jax.numpy as jnp
        import numpy as np
        B, N, QD = (4, 1024, 256)
        HEADS, DIM_HEAD = (8, 64)
        HID = HEADS * DIM_HEAD
        SCALE = DIM_HEAD ** (-0.5)
        key = jax.random.key(seed)
        ks = jax.random.split(key, 6)
        s_in = 1.0 / np.sqrt(QD)
        s_h = 1.0 / np.sqrt(HID)
        return {'x': jax.random.normal(ks[0], (B, N, QD), dtype=jnp.float32), 'Wq': jax.random.uniform(ks[1], (QD, HID), jnp.float32, -s_in, s_in), 'Wk': jax.random.uniform(ks[2], (QD, HID), jnp.float32, -s_in, s_in), 'Wv': jax.random.uniform(ks[3], (QD, HID), jnp.float32, -s_in, s_in), 'Wo': jax.random.uniform(ks[4], (HID, QD), jnp.float32, -s_h, s_h), 'bo': jax.random.uniform(ks[5], (QD,), jnp.float32, -s_h, s_h)}
    _L0_attn_all = _L0_attn_setup()
    _L0_attn_in = {k: v for k, v in _L0_attn_all.items() if k in ('Wq', 'Wk', 'Wv', 'Wo', 'bo')}
    del _L0_attn_all

    def _L0_xattn_setup():
        import jax, jax.numpy as jnp
        import numpy as np
        EMBED_DIM = 256
        HIDDEN_DIM = 256
        NUM_HEADS = 16
        CONTEXT_DIM = 192
        HEAD_DIM = EMBED_DIM // NUM_HEADS
        SCALE = HEAD_DIM ** (-0.5)

        def _split_heads(x):
            b, n, _ = x.shape
            return x.reshape(b, n, NUM_HEADS, -1).transpose(0, 2, 1, 3)
        key = jax.random.key(seed)
        ks = jax.random.split(key, 7)
        B, N, M = (4, 1024, 256)
        tokens = jax.random.normal(ks[0], (B, N, HIDDEN_DIM), dtype=jnp.float32)
        context = jax.random.normal(ks[1], (B, M, CONTEXT_DIM), dtype=jnp.float32)
        Wq = jax.random.normal(ks[2], (HIDDEN_DIM, EMBED_DIM), dtype=jnp.float32) * HIDDEN_DIM ** (-0.5)
        Wk = jax.random.normal(ks[3], (CONTEXT_DIM, EMBED_DIM), dtype=jnp.float32) * CONTEXT_DIM ** (-0.5)
        Wv = jax.random.normal(ks[4], (CONTEXT_DIM, HIDDEN_DIM), dtype=jnp.float32) * CONTEXT_DIM ** (-0.5)
        Wo = jax.random.normal(ks[5], (HIDDEN_DIM, HIDDEN_DIM), dtype=jnp.float32) * HIDDEN_DIM ** (-0.5)
        bo = jax.random.normal(ks[6], (HIDDEN_DIM,), dtype=jnp.float32) * 0.01
        return {'tokens': tokens, 'context': context, 'Wq': Wq, 'Wk': Wk, 'Wv': Wv, 'Wo': Wo, 'bo': bo}
    _L0_xattn_all = _L0_xattn_setup()
    _L0_xattn_in = {k: v for k, v in _L0_xattn_all.items() if k in ('Wq', 'Wk', 'Wv', 'Wo', 'bo')}
    del _L0_xattn_all

    def _L0_ffn_setup():
        import jax, jax.numpy as jnp
        import numpy as np
        D_MODEL, D_FF, RANK = (256, 1024, 64)
        B, S = (4, 1024)
        key = jax.random.key(seed)
        ks = jax.random.split(key, 7)
        return {'x': jax.random.normal(ks[0], (B, S, D_MODEL), dtype=jnp.float32), 'U1': jax.random.normal(ks[1], (D_MODEL, RANK), dtype=jnp.float32) * 0.02, 'V1': jax.random.normal(ks[2], (RANK, D_FF), dtype=jnp.float32) * 0.02, 'b1': jnp.zeros((D_FF,), dtype=jnp.float32), 'U2': jax.random.normal(ks[3], (D_FF, RANK), dtype=jnp.float32) * 0.02, 'V2': jax.random.normal(ks[4], (RANK, D_MODEL), dtype=jnp.float32) * 0.02, 'b2': jnp.zeros((D_MODEL,), dtype=jnp.float32)}
    _L0_ffn_all = _L0_ffn_setup()
    _L0_ffn_in = {k: v for k, v in _L0_ffn_all.items() if k in ('U1', 'V1', 'b1', 'U2', 'V2', 'b2')}
    del _L0_ffn_all
    return {'x': x, 'ctx_768': ctx_768, 'L0_attn_Wq': _L0_attn_in['Wq'], 'L0_attn_Wk': _L0_attn_in['Wk'], 'L0_attn_Wv': _L0_attn_in['Wv'], 'L0_attn_Wo': _L0_attn_in['Wo'], 'L0_attn_bo': _L0_attn_in['bo'], 'L0_xattn_Wq': _L0_xattn_in['Wq'], 'L0_xattn_Wk': _L0_xattn_in['Wk'], 'L0_xattn_Wv': _L0_xattn_in['Wv'], 'L0_xattn_Wo': _L0_xattn_in['Wo'], 'L0_xattn_bo': _L0_xattn_in['bo'], 'L0_ffn_U1': _L0_ffn_in['U1'], 'L0_ffn_V1': _L0_ffn_in['V1'], 'L0_ffn_b1': _L0_ffn_in['b1'], 'L0_ffn_U2': _L0_ffn_in['U2'], 'L0_ffn_V2': _L0_ffn_in['V2'], 'L0_ffn_b2': _L0_ffn_in['b2']}

def reference(x, ctx_768, L0_attn_Wq, L0_attn_Wk, L0_attn_Wv, L0_attn_Wo, L0_attn_bo, L0_xattn_Wq, L0_xattn_Wk, L0_xattn_Wv, L0_xattn_Wo, L0_xattn_bo, L0_ffn_U1, L0_ffn_V1, L0_ffn_b1, L0_ffn_U2, L0_ffn_V2, L0_ffn_b2):
    import jax
    import jax.numpy as jnp

    def _L0_attn_ref(x, Wq, Wk, Wv, Wo, bo):
        import jax, jax.numpy as jnp
        import numpy as np
        B, N, QD = (4, 1024, 256)
        HEADS, DIM_HEAD = (8, 64)
        HID = HEADS * DIM_HEAD
        SCALE = DIM_HEAD ** (-0.5)
        b, n, _ = x.shape
        q = x @ Wq
        k = x @ Wk
        v = x @ Wv

        def split_heads(t):
            return t.reshape(b, n, HEADS, DIM_HEAD).transpose(0, 2, 3, 1)
        q = split_heads(q)
        k = split_heads(k)
        v = split_heads(v)
        q = jax.nn.softmax(q, axis=-2) * SCALE
        k = jax.nn.softmax(k, axis=-1)
        context = jnp.einsum('bhdn,bhen->bhde', k, v)
        out = jnp.einsum('bhde,bhdn->bhen', context, q)
        out = out.transpose(0, 3, 1, 2).reshape(b, n, HID)
        return out @ Wo + bo

    def _L0_xattn_ref(tokens, context, Wq, Wk, Wv, Wo, bo):
        import jax, jax.numpy as jnp
        import numpy as np
        EMBED_DIM = 256
        HIDDEN_DIM = 256
        NUM_HEADS = 16
        CONTEXT_DIM = 192
        HEAD_DIM = EMBED_DIM // NUM_HEADS
        SCALE = HEAD_DIM ** (-0.5)

        def _split_heads(x):
            b, n, _ = x.shape
            return x.reshape(b, n, NUM_HEADS, -1).transpose(0, 2, 1, 3)
        Q = _split_heads(tokens @ Wq)
        K = _split_heads(context @ Wk)
        V = _split_heads(context @ Wv)
        scores = jnp.einsum('bhnd,bhmd->bhnm', Q, K) * SCALE
        attn = jax.nn.softmax(scores, axis=-1)
        out = jnp.einsum('bhnm,bhmd->bhnd', attn, V)
        b, h, n, d = out.shape
        out = out.transpose(0, 2, 1, 3).reshape(b, n, h * d)
        return out @ Wo + bo

    def _L0_ffn_ref(x, U1, V1, b1, U2, V2, b2):
        import jax, jax.numpy as jnp
        import numpy as np
        D_MODEL, D_FF, RANK = (256, 1024, 64)
        B, S = (4, 1024)
        P = jnp.einsum('bsd,dr->bsr', x, U1)
        H = jax.nn.gelu(jnp.einsum('bsr,rf->bsf', P, V1) + b1)
        Q = jnp.einsum('bsf,fr->bsr', H, U2)
        return jnp.einsum('bsr,rd->bsd', Q, V2) + b2
    x = _layernorm(x + _L0_attn_ref(x, L0_attn_Wq, L0_attn_Wk, L0_attn_Wv, L0_attn_Wo, L0_attn_bo), axis=-1)
    x = _layernorm(x + _L0_xattn_ref(x, ctx_768, L0_xattn_Wq, L0_xattn_Wk, L0_xattn_Wv, L0_xattn_Wo, L0_xattn_bo), axis=-1)
    x = _layernorm(x + _L0_ffn_ref(x, L0_ffn_U1, L0_ffn_V1, L0_ffn_b1, L0_ffn_U2, L0_ffn_V2, L0_ffn_b2), axis=-1)
    return x

_drawn_inputs = setup_inputs


def setup_inputs(seed=0):
    import zlib

    import numpy as np

    out = dict(_drawn_inputs(seed))
    spreads = {'L0_ffn_b1': (0.0, 0.8), 'L0_ffn_b2': (0.0, 0.8)}
    factors = {'L0_attn_Wq': 8.0,
     'L0_attn_Wk': 8.0,
     'L0_attn_Wv': 8.0,
     'L0_attn_Wo': 8.0,
     'L0_xattn_bo': 6.177,
     'L0_ffn_U1': 8.0,
     'L0_ffn_V1': 8.0,
     'L0_ffn_U2': 8.0,
     'L0_ffn_V2': 8.0,
     'L0_attn_bo': 3.837}
    for name, (base, spread) in spreads.items():
        noise = np.random.default_rng([zlib.crc32(name.encode()), seed]).standard_normal(out[name].shape)
        drawn = base * np.exp(spread * noise) if base else spread * noise
        out[name] = jnp.asarray(drawn.astype(out[name].dtype))
    for name, factor in factors.items():
        out[name] = (out[name] * factor).astype(out[name].dtype)
    return out
```

```python
from contextlib import ExitStack

import concourse.bass as bass
from concourse import mybir

F32 = mybir.dt.float32
BF16 = mybir.dt.bfloat16
ALU = mybir.AluOpType
ACT = mybir.ActivationFunctionType
AX = mybir.AxisListType

P = 128
EPS = 1e-5
GELU_CUBIC = 0.044715
GELU_SCALE = 0.7978845608028654

STAGE1_AT = {
    1: [("cT", 0), ("cT", 1)],
    2: [("kX", 0), ("kX", 1)],
    3: [("vX", 0), ("vX", 1)],
    4: [("xT", 0), ("xT", 1)],
    5: [("k", 0), ("q", 0)],
    6: [("k", 1), ("q", 1)],
    7: [("k", 2), ("qT", 0)],
    8: [("k", 3), ("q", 2)],
    9: [("ek", 0), ("qT", 1)],
    10: [("ek", 1), ("q", 3)],
    11: [("ek", 2), ("qT", 2)],
    12: [("ek", 3), ("xTk", 0)],
    13: [("xTk", 1), ("qT", 3), ("ctx", 0)],
    14: [("G", 0), ("G", 1)],
    15: [("o", 0), ("o", 1)],
    17: [("x1T", 0), ("x1T", 1)],
    18: [("qX", 0), ("qX", 1)],
}
Q_SUM_AT = {("q", 1): 0, ("qT", 0): 1, ("qT", 1): 2, ("qT", 2): 3}
STAGE2_AT = {
    1: ("oT", 0), 2: ("oT", 1), 3: ("y", 0), 4: ("y", 1), 6: ("x2T", 0), 7: ("x2T", 1), 8: ("f1", 0),
    9: ("f2", 0), 10: ("f2", 1), 11: ("f2", 2), 12: ("f2", 3), 13: ("f3", 0),
    14: ("f2", 4), 15: ("f2", 5), 16: ("f2", 6), 17: ("f2", 7), 18: ("f3", 1), 19: ("f4", 0), 20: ("f4", 1),
}
SLOTS = 22
EXP_LAG = 6


class Batch:

    def __init__(self, off, loop=None):
        self.off, self.loop = off, loop

    def shifted(self, by):
        return Batch(self.off + by, self.loop)

    @property
    def parity(self):
        return self.off % 2

    @property
    def first(self):
        return self.loop is None and self.off == 0

    def index(self):
        return self.off if self.loop is None else self.loop * 2 + self.off

    def count(self, per_batch, more):
        if self.loop is None:
            return self.off * per_batch + more
        return self.loop * (2 * per_batch) + (self.off * per_batch + more)


class Ring:

    def __init__(self, order, banks, full, free):
        self.place = {name: (n % len(banks), n // len(banks)) for n, name in enumerate(order)}
        self.uses = [len(order[i::len(banks)]) for i in range(len(banks))]
        self.banks, self.full, self.free = banks, full, free

    def bank(self, name):
        return self.banks[self.place[name][0]]

    def sem_full(self, name):
        return self.full[self.place[name][0]]

    def sem_free(self, name):
        return self.free[self.place[name][0]]

    def fills(self, name, batch):
        i, k = self.place[name]
        return batch.count(self.uses[i], k + 1)

    def frees(self, name, batch):
        i, k = self.place[name]
        return batch.count(self.uses[i], k + 1)

    def reads(self, name, batch):
        i, k = self.place[name]
        return batch.count(self.uses[i], k + 2)

    def all_read(self, names, batch, then=None):
        need = {}
        for name in names:
            i, k = self.place[name]
            need[i] = max(need.get(i, 0), k + 2)
        if then is not None:
            i, k = self.place[then]
            need[i] = max(need.get(i, 0), k + 1)
        return [(self.free[i], batch.count(self.uses[i], k)) for i, k in need.items()]


def decoder_layer(nc, x, ctx_768, a_wq, a_wk, a_wv, a_wo, a_bo, c_wq, c_wk, c_wv, c_wo, c_bo,
                  u1, v1, b1, u2, v2, b2, out):
    B, N, D = x.shape
    M, CD = ctx_768.shape[1:]
    HID = a_wq.shape[1]
    DH = 64
    HEADS, HD = 16, D // 16
    R, F = v1.shape
    T = N // P
    C = D // P
    J = HID // P
    GR = HEADS // 4
    NF = F // P
    UNITS = GR * T
    PARTS = 3 * HD
    PROD = 6 * HD
    assert (N, M, D, HID, R, T, C, J) == (512, 512, 256, 512, 64, 4, 2, 4) and B % 2 == 0 and CD == 192

    x_v = x.rearrange("b (p t) d -> b p t d", t=T)
    c_v = ctx_768.rearrange("b (p t) d -> b p t d", t=T)
    out_v = out.rearrange("b (p t) d -> b p t d", t=T)
    q_parts = nc.dram_tensor("q_parts", [HEADS, PARTS, N], BF16, kind="Internal").ap()
    k_parts = nc.dram_tensor("k_parts", [HEADS, PARTS, M], BF16, kind="Internal").ap()

    es = ExitStack()
    with es:
        def sb(name, shape, dt=F32):
            return es.enter_context(nc.sbuf_tensor(name, shape, dt))

        def sem(name):
            return es.enter_context(nc.semaphore(name))

        def sems(name, n):
            return [sem(f"{name}{i}") for i in range(n)]

        wq_a, wk_a, wv_a = sb("wq_a", [P, C, HID]), sb("wk_a", [P, C, HID]), sb("wv_a", [P, C, HID])
        wo_a = sb("wo_a", [P, J, D])
        wq_c, wk_c, wv_c, wo_c = (sb(n, [P, C, D]) for n in ("wq_c", "wk_c", "wv_c", "wo_c"))
        u1_s, v1_s = sb("u1_s", [P, C, R]), sb("v1_s", [R, F])
        u2_s, v2_s = sb("u2_s", [P, NF, R]), sb("v2_s", [2 * R, D])
        b1_s = sb("b1_s", [P, NF])
        bo_a, bo_c, b2_s = sb("bo_a", [P, D]), sb("bo_c", [P, D]), sb("b2_s", [P, D])
        ident = sb("ident", [P, P])
        minus_half = sb("minus_half", [P, T])

        x_s = sb("x_s", [P, T, D])
        c_s = sb("c_s", [P, T, CD])
        tokT = sb("tokT", [P, C, N])
        ekT = sb("ekT", [P, J, N])
        ek = sb("ek", [P, T, HID])
        kneg, ksum, krec = sb("kneg", [P, J]), sb("ksum", [P, J]), sb("krec", [P, J])
        xTk = sb("xTk", [P, C, HID])
        ctxT = sb("ctxT", [P, J, P])
        G = sb("G", [P, J, D])
        qw = sb("qw", [P, 2, HID])
        qmax, qsum, qrec = (sb(n, [P, 2, HID // DH]) for n in ("qmax", "qsum", "qrec"))
        qT = sb("qT", [P, J, N])
        x1 = sb("x1", [P, T, D])
        st1, mv1, sd1, rs1 = sb("st1", [P, T, 6]), sb("mv1", [P, T, 2]), sb("sd1", [P, T]), sb("rs1", [P, T])
        part = sb("part", [P, 2, 3, N], BF16)
        rest = sb("rest", [P, 2, N])
        x1b = sb("x1b", [P, 2, T, D])
        vX = sb("vX", [P, 2, T, HEADS, HD + 1])
        QS = sb("QS", [P, HEADS, N], BF16)
        KS = sb("KS", [P, HEADS, M], BF16)
        mx = sb("mx", [P, GR, 4, T])
        mpart = sb("mpart", [4 * T, 2, 3, P], BF16)
        mrest = sb("mrest", [4 * T, 2, P])
        probs = sb("probs", [P, 8, N])
        oTs = sb("oTs", [P, N])
        orec = sb("orec", [P, T, 4])
        oN = sb("oN", [P, T, D])
        oT = sb("oT", [P, C, N])
        x2 = sb("x2", [P, T, D])
        x2T = sb("x2T", [P, C, N])
        st2, mv2, sd2, rs2 = sb("st2", [P, T, 6]), sb("mv2", [P, T, 2]), sb("sd2", [P, T]), sb("rs2", [P, T])
        pT = sb("pT", [R, N])
        hu, hv = sb("hu", [P, 2, N]), sb("hv", [P, 2, N])
        h = sb("h", [P, 4, N])
        r2 = sb("r2", [2 * R, N])

        def banks(name, n):
            return [es.enter_context(nc.psum_tensor(f"{name}{i}", [P, 512], F32)) for i in range(n)]

        order1 = [name for s in sorted(STAGE1_AT) for name in STAGE1_AT[s]]
        order2 = [STAGE2_AT[s] for s in sorted(STAGE2_AT)]
        order_max = []
        for s in range(4 * GR + 1):
            order_max += [("s", s, i) for i in range(4)] if s < 4 * GR else []
            order_max += [("m", s // 4 - 1)] if s % 4 == 0 and s else []
        order_exp = [("e", u, i) for u in range(UNITS) for i in range(4)]
        ring1 = Ring(order1, banks("ps_one", 2), sems("one_full", 2), sems("one_read", 2))
        ring2 = Ring(order2, banks("ps_two", 1), sems("two_full", 1), sems("two_read", 1))
        ring_max = Ring(order_max, banks("ps_max", 2), sems("max_full", 2), sems("max_read", 2))
        ring_exp = Ring(order_exp, banks("ps_exp", 2), sems("exp_full", 2), sems("exp_read", 2))
        ps_av = banks("ps_av", 1)[0]

        w_loaded, const_ready, diag_ready, init_ready = sem("w_loaded"), sem("const_ready"), sem("diag_ready"), sem("init_ready")
        rows_loaded = sem("rows_loaded")
        sp_alone, pool_alone, dve_alone, pe_alone = (sem(n) for n in ("sp_alone", "pool_alone", "dve_alone", "pe_alone"))
        x_loaded, c_loaded, stored = sem("x_loaded"), sem("c_loaded"), sem("stored")
        parts_written = sems("parts_written", 2)
        stack_loaded = sems("stack_loaded", GR)
        maxrow_loaded = sems("maxrow_loaded", GR)
        kneg_ready, krec_ready = sem("kneg_ready"), sem("krec_ready")
        qmax_ready, qexp_ready, qsum_ready, qrec_ready, qn_ready = (sem(n) for n in (
            "qmax_ready", "qexp_ready", "qsum_ready", "qrec_ready", "qn_ready"))
        resid_ready = sem("resid_ready")
        stat1, mean1, sd1_ready, rs1_ready, x1_ready, x1b_ready = (sem(n) for n in (
            "stat1", "mean1", "sd1_ready", "rs1_ready", "x1_ready", "x1b_ready"))
        hi_ready, mid_ready, lo_ready = sem("hi_ready"), sem("mid_ready"), sem("lo_ready")
        mhi_ready, mrest_ready, mmid_ready, mlo_ready = (sem(n) for n in (
            "mhi_ready", "mrest_ready", "mmid_ready", "mlo_ready"))
        av_done = sem("av_done")
        o_copied, o_turned, orec_ready, o_ready = (sem(n) for n in ("o_copied", "o_turned", "orec_ready", "o_ready"))
        resid2_ready = sem("resid2_ready")
        stat2, mean2, sd2_ready, rs2_ready, x2_ready = (sem(n) for n in (
            "stat2", "mean2", "sd2_ready", "rs2_ready", "x2_ready"))
        hu_ready, hv_ready, tanh_ready, h_ready = sem("hu_ready"), sem("hv_ready"), sem("tanh_ready"), sem("h_ready")

        N_WEIGHTS = 16

        def unit_group(u):
            return u // T, u % T

        block = es.enter_context(nc.Block())

        def run(engine, slot):
            for s in range(SLOTS):
                slot(s, None, Batch(0), None)
            for s in range(SLOTS):
                slot(s, Batch(0), Batch(1), None)
            with engine.Fori(0, (B - 2) // 2) as i:
                for off in (1, 2):
                    b = Batch(off, i)
                    for s in range(SLOTS):
                        slot(s, b, b.shifted(1), b.shifted(-1))
            for s in range(SLOTS):
                slot(s, Batch(B - 1), None, Batch(B - 2))
            for s in range(SLOTS):
                slot(s, None, None, Batch(B - 1))

        @block.sync
        def _(sp):
            for n, (dst, src) in enumerate([
                (wk_c[:], c_wk), (wv_c[:], c_wv),
                (wk_a[:], a_wk), (wq_a[:], a_wq), (wv_a[:], a_wv), (wo_a[:], a_wo), (wq_c[:], c_wq),
                (wo_c[:], c_wo), (u1_s[:], u1), (v1_s[:], v1), (u2_s[:], u2)]):
                if n < 2:
                    sp.dma_start(dst[:, 0, :], src[0:P, :]).then_inc(w_loaded, 16)
                    sp.dma_start(dst[0:CD - P, 1, :], src[P:CD, :]).then_inc(w_loaded, 16)
                elif src is u2:
                    sp.dma_start(dst, src.rearrange("(p f) r -> p f r", p=P)).then_inc(w_loaded, 16)
                elif dst.shape[0] == P:
                    sp.dma_start(dst, src.rearrange("(c p) n -> p c n", p=P)).then_inc(w_loaded, 16)
                else:
                    sp.dma_start(dst, src).then_inc(w_loaded, 16)
            for half in range(2):
                sp.dma_start(v2_s[half * R:(half + 1) * R, :], v2).then_inc(w_loaded, 16)
            sp.dma_start(b1_s[:], b1.rearrange("(p f) -> p f", p=P)).then_inc(w_loaded, 16)

            def stack_in(g, b):
                for c in range(2):
                    if g // 2 == c:
                        sp.wait_ge(parts_written[c], b.count(96, 96))
                        sp.sem_inc(sp_alone, 1)
                hs = slice(4 * g, 4 * g + 4)
                for dst, src, first in ((QS, q_parts, 0), (KS, k_parts, 1)):
                    for row, rows in ((0, 3), (3, 2), (5, 1)):
                        at = (3 - rows) * HD if first else 0
                        sp.dma_start(dst[row * HD:(row + rows) * HD, hs, :],
                                     src[hs, at:at + rows * HD, :].rearrange("h r n -> r h n")).then_inc(stack_loaded[g], 16)

            def parts_out(c, which, b):
                k = 2 * which + c
                sp.wait_ge(lo_ready, b.count(4, k + 1))
                sp.sem_inc(sp_alone, 1)
                if which == 0:
                    for g in range(GR):
                        if not b.first:
                            sp.wait_ge(stack_loaded[g], b.count(96, 0))
                            sp.sem_inc(sp_alone, 1)
                dst = (k_parts, q_parts)[which]
                for i in range(3):
                    at = (i if which else 2 - i) * HD
                    sp.dma_start(dst[8 * c:8 * c + 8, at:at + HD, :], part[:, c, i, :]).then_inc(parts_written[c], 16)

            def slot(s, bx, b1_, b2_):
                if b1_ is not None and s == 0:
                    if not b1_.first:
                        sp.wait_ge(ring1.sem_full(("cT", 1)), ring1.fills(("cT", 1), b1_.shifted(-1)))
                        sp.sem_inc(sp_alone, 1)
                    sp.dma_start(c_s[:], c_v[b1_.index()]).then_inc(c_loaded, 16)
                    if not b1_.first:
                        sp.wait_ge(ring1.sem_full(("xTk", 0)), ring1.fills(("xTk", 0), b1_.shifted(-1)))
                        sp.sem_inc(sp_alone, 1)
                    if not b1_.first:
                        sp.wait_ge(ring1.sem_full(("xTk", 1)), ring1.fills(("xTk", 1), b1_.shifted(-1)))
                        sp.sem_inc(sp_alone, 1)
                    if not b1_.first:
                        sp.wait_ge(resid_ready, b1_.count(1, 0))
                        sp.sem_inc(sp_alone, 1)
                    sp.dma_start(x_s[:], x_v[b1_.index()]).then_inc(x_loaded, 16)
                if b1_ is not None:
                    names = STAGE1_AT.get(s, [])
                    for name in names:
                        if name in (("kX", 0), ("kX", 1)):
                            parts_out(name[1], 0, b1_)
                        if name in (("qX", 0), ("qX", 1)):
                            parts_out(name[1], 1, b1_)
                if bx is not None and s % 4 == 0 and s >= 4 and s // 4 - 1 < GR:
                    g = s // 4 - 1
                    sp.wait_ge(mlo_ready, bx.count(GR, g + 1))
                    sp.sem_inc(sp_alone, 1)
                    for i in range(3):
                        sp.dma_start(QS[PROD + i:PROD + i + 1, 4 * g:4 * g + 4, :].rearrange("a h (t n) -> a (h t) n", n=P),
                                     mpart[:, g % 2, i, :]).then_inc(maxrow_loaded[g], 16)
                if b2_ is not None and s == 20:
                    sp.wait_ge(x2_ready, b2_.count(8, 8))
                    sp.sem_inc(sp_alone, 1)
                    sp.dma_start(out_v[b2_.index()], x2[:]).then_inc(stored, 16)
                if b1_ is not None and s == SLOTS - 1:
                    for g in range(GR):
                        if bx is not None:
                            sp.wait_ge(ring_exp.sem_full(("e", 4 * g + 3, 2)), ring_exp.fills(("e", 4 * g + 3, 2), bx))
                            sp.sem_inc(sp_alone, 1)
                            sp.wait_ge(ring_exp.sem_full(("e", 4 * g + 3, 3)), ring_exp.fills(("e", 4 * g + 3, 3), bx))
                            sp.sem_inc(sp_alone, 1)
                        stack_in(g, b1_)

            run(sp, slot)
            sp.wait_ge(stored, 16 * (B + 1))

        @block.tensor
        def _(pe):
            pe.wait_ge(w_loaded, 16 * N_WEIGHTS)
            pe.wait_ge(diag_ready, 1)
            pe.wait_ge(init_ready, 1)

            def mm(dst, lhsT, rhs, start, stop, **kw):
                return nc.tensor.matmul(dst, lhsT, rhs, start=start, stop=stop, **kw)

            def transpose(dst, src):
                return nc.tensor.transpose(dst, src, ident[0:src.shape[0], 0:src.shape[0]])

            def tile(t):
                return slice(t * P, (t + 1) * P)

            needs1 = {"kX": [("cT", 0), ("cT", 1)], "vX": [("cT", 0), ("cT", 1)], "k": [("xT", 0), ("xT", 1)],
                      "q": [("xT", 0), ("xT", 1)], "ek": [("k", j) for j in range(J)], "xTk": [("ek", t) for t in range(T)],
                      "ctx": [("xTk", c) for c in range(C)], "G": [("ctx", 0)],
                      "o": [("G", 0), ("G", 1)] + [("qT", t) for t in range(T)], "qX": [("x1T", 0), ("x1T", 1)]}
            needs2 = {"y": [("oT", 0), ("oT", 1)], "f1": [("x2T", 0), ("x2T", 1)], "f2": [("f1", 0)], "f4": [("f3", 1)]}

            def stage1(name, b):
                kind, k = name
                ps = ring1.bank(name)
                if name == ("cT", 0):
                    pe.wait_ge(c_loaded, b.count(16, 16))
                if name == ("xT", 0):
                    pe.wait_ge(x_loaded, b.count(16, 16))
                if kind == "qT":
                    pe.wait_ge(qn_ready, b.count(T, k + 1))
                if kind == "x1T":
                    pe.wait_ge(x1_ready, b.count(T, T))
                for read, count in ring1.all_read(needs1.get(kind, []), b, then=name):
                    pe.wait_ge(read, count)
                if name == ("cT", 1):
                    pe.sem_inc(pe_alone, 1)
                if kind == "cT":
                    rows = P if k == 0 else CD - P
                    for t in range(T):
                        last = transpose(ps[0:rows, tile(t)], c_s[:, t, k * P:k * P + rows])
                if kind in ("kX", "qX"):
                    w = wk_c if kind == "kX" else wq_c
                    for c in range(2):
                        rows = CD - P if kind == "kX" and c == 1 else P
                        last = mm(ps[:], w[0:rows, c, k * P:(k + 1) * P], tokT[0:rows, c, :], c == 0, c == 1)
                if kind == "vX":
                    for i in range(2):
                        for c in range(2):
                            rows = CD - P if c == 1 else P
                            last = mm(ps[:, i * D:(i + 1) * D], tokT[0:rows, c, tile(2 * k + i)], wv_c[0:rows, c, :],
                                      c == 0, c == 1)
                if kind in ("xT", "x1T"):
                    src = x_s if kind == "xT" else x1
                    for t in range(T):
                        last = transpose(ps[:, tile(t)], src[:, t, k * P:(k + 1) * P])
                if kind == "k":
                    for c in range(C):
                        last = mm(ps[:], wk_a[:, c, tile(k)], tokT[:, c, :], c == 0, c == C - 1)
                if kind == "q":
                    for c in range(C):
                        last = mm(ps[:], tokT[:, c, tile(k)], wq_a[:, c, :], c == 0, c == C - 1)
                if kind == "ek":
                    for j in range(J):
                        last = transpose(ps[:, tile(j)], ekT[:, j, tile(k)])
                if kind == "xTk":
                    for t in range(T):
                        last = mm(ps[:], x_s[:, t, k * P:(k + 1) * P], ek[:, t, :], t == 0, t == T - 1)
                if kind == "ctx":
                    for j in range(J):
                        for c in range(C):
                            last = mm(ps[:, tile(j)], wv_a[:, c, tile(j)], xTk[:, c, tile(j)], c == 0, c == C - 1)
                if kind == "G":
                    for i in range(2):
                        last = mm(ps[:, i * D:(i + 1) * D], ctxT[:, 2 * k + i, :], wo_a[:, 2 * k + i, :], True, True)
                if kind == "qT":
                    for j in range(J):
                        last = transpose(ps[:, tile(j)], qw[:, k % 2, tile(j)])
                if kind == "o":
                    for i in range(2):
                        for j in range(J):
                            last = mm(ps[:, i * D:(i + 1) * D], qT[:, j, tile(2 * k + i)], G[:, j, :], j == 0, j == J - 1)
                last.then_inc(ring1.sem_full(name), 1)

            def stage2(name, b):
                kind, k = name
                ps = ring2.bank(name)
                if kind == "oT":
                    pe.wait_ge(o_ready, b.count(GR, GR))
                if kind == "x2T":
                    pe.wait_ge(x2_ready, b.count(2 * T, T))
                if kind == "f3":
                    pe.wait_ge(h_ready, b.count(NF, 4 * k + 4))
                for read, count in ring2.all_read(needs2.get(kind, []), b, then=name):
                    pe.wait_ge(read, count)
                if kind in ("oT", "x2T"):
                    src = oN if kind == "oT" else x2
                    for t in range(T):
                        last = transpose(ps[:, tile(t)], src[:, t, k * P:(k + 1) * P])
                if kind == "y":
                    for i in range(2):
                        for c in range(C):
                            last = mm(ps[:, i * D:(i + 1) * D], oT[:, c, tile(2 * k + i)], wo_c[:, c, :], c == 0, c == C - 1)
                if kind == "f1":
                    for c in range(C):
                        last = mm(ps[0:R, :], u1_s[:, c, :], x2T[:, c, :], c == 0, c == C - 1)
                if kind == "f2":
                    last = mm(ps[:], v1_s[:, k::NF], pT[:], True, True)
                if kind == "f3":
                    for i in range(4):
                        half = i % 2
                        last = mm(ps[half * R:(half + 1) * R, :], u2_s[:, 4 * k + i, :], h[:, i, :], i < 2, i >= 2)
                if kind == "f4":
                    for i in range(2):
                        last = mm(ps[:, i * D:(i + 1) * D], r2[:, tile(2 * k + i)], v2_s[:], True, True)
                last.then_inc(ring2.sem_full(name), 1)

            def scores_for_max(s, i, b):
                g, t = unit_group(s)
                name, head = ("s", s, i), 4 * g + i
                if i == 0 and t == 0:
                    pe.wait_ge(stack_loaded[g], b.count(96, 96))
                pe.wait_ge(ring_max.sem_free(name), ring_max.frees(name, b))
                mm(ring_max.bank(name)[:], QS[0:PROD, head, tile(t)], KS[0:PROD, head, :], True, True)\
                    .then_inc(ring_max.sem_full(name), 1)

            def turn_max(g, b):
                name = ("m", g)
                for read, count in ring_max.all_read([("s", 4 * g + 3, 2), ("s", 4 * g + 3, 3)], b, then=name):
                    pe.wait_ge(read, count)
                transpose(ring_max.bank(name)[0:4 * T, 0:P], mx[:, g, :, :].rearrange("p h t -> p (h t)"))\
                    .then_inc(ring_max.sem_full(name), 1)

            def scores_for_exp(u, i, b):
                g, mc = unit_group(u)
                name, head = ("e", u, i), 4 * g + i
                if i == 0 and mc == 0:
                    pe.wait_ge(maxrow_loaded[g], b.count(48, 48))
                pe.wait_ge(ring_exp.sem_free(name), ring_exp.frees(name, b))
                mm(ring_exp.bank(name)[:], KS[0:PROD + 3, head, tile(mc)], QS[0:PROD + 3, head, :], True, True)\
                    .then_inc(ring_exp.sem_full(name), 1)

            def probs_times_v(u, b):
                g, mc = unit_group(u)
                if mc == 0:
                    if g or not b.first:
                        pe.wait_ge(o_ready, b.count(GR, g))
                    if g == 0:
                        for read, count in ring1.all_read([("vX", 0), ("vX", 1)], b):
                            pe.wait_ge(read, count)
                for read, count in ring_exp.all_read([("e", u, i) for i in range(4)], b):
                    pe.wait_ge(read, count)
                for i in range(4):
                    last = mm(ps_av[32 * i:32 * i + HD + 1, :], vX[:, b.parity, mc, 4 * g + i, :],
                              probs[:, 4 * (u % 2) + i, :], mc == 0, mc == T - 1, tile_position=(0, 32 * i))
                last.then_inc(av_done, 1)

            def turn_o(g, b):
                pe.wait_ge(o_copied, b.count(GR, g + 1))
                for t in range(T):
                    last = transpose(ps_av[:, tile(t)], oTs[:, tile(t)])
                last.then_inc(o_turned, 1)

            def slot(s, bx, b1_, b2_):
                ones = STAGE1_AT.get(s, []) if b1_ is not None else []
                u = s - EXP_LAG
                for i in range(2):
                    if bx is not None and s < UNITS:
                        scores_for_max(s, i, bx)
                if bx is not None and s >= EXP_LAG + 5 and (s - EXP_LAG - 5) % 4 == 0:
                    turn_o((s - EXP_LAG - 5) // 4, bx)
                if b2_ is not None and s == 0:
                    probs_times_v(UNITS - 1, b2_)
                for name in ones[:1]:
                    stage1(name, b1_)
                for i in range(2, 4):
                    if bx is not None and s < UNITS:
                        scores_for_max(s, i, bx)
                if bx is not None and s % 4 == 0 and 4 <= s <= UNITS:
                    turn_max(s // 4 - 1, bx)
                for i in range(2):
                    if bx is not None and 0 <= u < UNITS:
                        scores_for_exp(u, i, bx)
                if b2_ is not None and s == 0:
                    turn_o(GR - 1, b2_)
                for name in ones[1:]:
                    stage1(name, b1_)
                for i in range(2, 4):
                    if bx is not None and 0 <= u < UNITS:
                        scores_for_exp(u, i, bx)
                if b2_ is not None and s in STAGE2_AT:
                    stage2(STAGE2_AT[s], b2_)
                if bx is not None and 1 <= u <= UNITS - 1:
                    probs_times_v(u - 1, bx)

            run(pe, slot)

        @block.scalar
        def _(act):
            def stage1(name, b):
                kind, k = name
                ps = ring1.bank(name)
                if kind in ("G", "o", "q", "cT_"):
                    return
                act.wait_ge(ring1.sem_full(name), ring1.fills(name, b))
                if kind in ("cT", "xT", "x1T"):
                    rows = CD - P if name == ("cT", 1) else P
                    nc.scalar.activation(tokT[0:rows, k, :], ps[0:rows, :], ACT.Copy).then_inc(ring1.sem_free(name), 1)
                if kind in ("kX", "qX"):
                    n = k + (2 if kind == "qX" else 0)
                    if n >= 2:
                        act.wait_ge(parts_written[k], b.count(96, 48))
                    else:
                        if not b.first:
                            act.wait_ge(parts_written[k], b.count(96, 0))
                    nc.scalar.activation(part[:, k, 0, :], ps[:], ACT.Copy, scale=HD ** -0.5 if kind == "qX" else 1.0)\
                        .then_inc(hi_ready, 1)
                if kind == "vX":
                    nc.scalar.activation(vX[:, b.parity, 2 * k:2 * k + 2, :, 0:HD],
                                         ps[:].rearrange("p (t h d) -> p t h d", t=2, h=HEADS), ACT.Copy)\
                        .then_inc(ring1.sem_free(name), 1)
                if kind == "k":
                    act.wait_ge(kneg_ready, b.count(J, k + 1))
                    nc.scalar.activation(ekT[:, k, :], ps[:], ACT.Exp, bias=kneg[:, k:k + 1], accum_out=ksum[:, k:k + 1])\
                        .then_inc(ring1.sem_free(name), 1)
                if kind in ("ek", "xTk"):
                    dst = ek if kind == "ek" else xTk
                    nc.scalar.activation(dst[:, k, :], ps[:], ACT.Copy).then_inc(ring1.sem_free(name), 1)
                if kind == "ctx":
                    for i in range(2):
                        at = slice(i * DH, (i + 1) * DH)
                        last = nc.scalar.activation(ctxT[at, :, at], ps[at, :].rearrange("p (j d) -> p j d", d=P)[:, :, at],
                                                    ACT.Copy)
                    last.then_inc(ring1.sem_free(name), 1)
                if kind == "qT":
                    nc.scalar.activation(qT[:, :, k * P:(k + 1) * P], ps[:].rearrange("p (j n) -> p j n", n=P), ACT.Copy)\
                        .then_inc(ring1.sem_free(name), 1)

            def exp_q(t, b):
                act.wait_ge(ring1.sem_free(("q", t)), ring1.reads(("q", t), b))
                nc.scalar.activation(qw[:, t % 2, :], qw[:, t % 2, :], ACT.Exp).then_inc(qexp_ready, 1)

            def stage2(name, b):
                kind, k = name
                ps = ring2.bank(name)
                if kind in ("y", "f4") or name == ("f3", 1):
                    return
                act.wait_ge(ring2.sem_full(name), ring2.fills(name, b))
                free = ring2.sem_free(name)
                if kind in ("oT", "x2T"):
                    dst = oT if kind == "oT" else x2T
                    nc.scalar.activation(dst[:, k, :], ps[:], ACT.Copy).then_inc(free, 1)
                if kind == "f1":
                    nc.scalar.activation(pT[:], ps[0:R, :], ACT.Copy).then_inc(free, 1)
                if kind == "f2":
                    if k >= 2:
                        act.wait_ge(h_ready, b.count(NF, k - 1))
                    nc.scalar.activation(hu[:, k % 2, :], ps[:], ACT.Identity, bias=b1_s[:, k:k + 1]).then_inc(hu_ready, 1)
                    nc.scalar.activation(hv[:, k % 2, :], ps[:], ACT.Square, bias=b1_s[:, k:k + 1]).then_inc(free, 1)
                if kind == "f3":
                    nc.scalar.activation(r2[:], ps[:], ACT.Copy, scale=0.5).then_inc(free, 1)

            def stage2_late(name, b):
                kind, k = name
                if kind == "f2":
                    act.wait_ge(hv_ready, b.count(NF, k + 1))
                    nc.scalar.activation(hv[:, k % 2, :], hv[:, k % 2, :], ACT.Tanh, scale=GELU_SCALE * GELU_CUBIC)\
                        .then_inc(tanh_ready, 1)

            def exp_scores(u, i, b):
                name = ("e", u, i)
                if u >= 2 or not b.first:
                    act.wait_ge(av_done, b.count(UNITS, u - 1))
                act.wait_ge(ring_exp.sem_full(name), ring_exp.fills(name, b))
                nc.scalar.activation(probs[:, 4 * (u % 2) + i, :], ring_exp.bank(name)[:], ACT.Exp)\
                    .then_inc(ring_exp.sem_free(name), 1)

            def copy_o(g, b):
                act.wait_ge(av_done, b.count(UNITS, 4 * (g + 1)))
                nc.scalar.activation(oTs[:], ps_av[:], ACT.Copy).then_inc(o_copied, 1)

            act.wait_ge(w_loaded, 16 * N_WEIGHTS)
            act.wait_ge(init_ready, 1)

            def slot(s, bx, b1_, b2_):
                ones = STAGE1_AT.get(s, []) if b1_ is not None else []
                u = s - EXP_LAG
                if bx is not None and s >= EXP_LAG + 5 and (s - EXP_LAG - 5) % 4 == 0:
                    copy_o((s - EXP_LAG - 5) // 4, bx)
                if b2_ is not None and s == 0:
                    copy_o(GR - 1, b2_)
                for name in ones[:1]:
                    stage1(name, b1_)
                for i in range(2):
                    if bx is not None and 0 <= u < UNITS:
                        exp_scores(u, i, bx)
                for name in ones[1:]:
                    stage1(name, b1_)
                for i in range(2, 4):
                    if bx is not None and 0 <= u < UNITS:
                        exp_scores(u, i, bx)
                for kind, k in ones:
                    if kind == "q":
                        exp_q(k, b1_)
                if b2_ is not None and s in STAGE2_AT:
                    stage2(STAGE2_AT[s], b2_)
                    stage2_late(STAGE2_AT[s], b2_)

            run(act, slot)

        @block.vector
        def _(dve):
            for ring in (ring1, ring2, ring_max, ring_exp):
                for free in ring.free:
                    dve.sem_inc(free, 1)
            dve.sem_inc(stored, 16)
            nc.vector.memset(ps_av[:], 0.0)
            nc.vector.memset(ctxT[:], 0.0)
            nc.vector.memset(KS[PROD:PROD + 3, :, :], 1.0)
            nc.vector.memset(minus_half[:], -0.5)
            nc.vector.memset(vX[:, :, :, :, HD:HD + 1], 1.0).then_inc(init_ready, 1)
            dve.wait_ge(w_loaded, 16 * N_WEIGHTS)

            def layernorm_stats(z, st, mv, k, s_stat, s_mean, b, per, base):
                for i in range(2):
                    t = 2 * k + i
                    nc.vector.bn_stats(out=st[:, t, :], in_=z[:, t, :]).then_inc(s_stat, 1)
                for i in range(2):
                    t = 2 * k + i
                    dve.wait_ge(s_stat, b.count(per, base + t + 1))
                    dve.sem_inc(dve_alone, 1)
                    nc.vector.bn_aggr(out=mv[:, t, :], in_=st[:, t, :]).then_inc(s_mean, 1)

            def normalise(z, mv, rs, s_done):
                for t in range(T):
                    nc.vector.tensor_scalar(z[:, t, :], z[:, t, :], mv[:, t, 0:1], rs[:, t:t + 1], ALU.subtract, ALU.mult)\
                        .then_inc(s_done, 1)

            def stage1(name, b):
                kind, k = name
                ps = ring1.bank(name)
                if name in Q_SUM_AT:
                    sum_q(Q_SUM_AT[name], b)
                if kind == "k":
                    dve.wait_ge(ring1.sem_full(name), ring1.fills(name, b))
                    nc.vector.tensor_reduce(kneg[:, k:k + 1], ps[:], axis=AX.X, op=ALU.max, negate=True).then_inc(kneg_ready, 1)
                if kind == "q":
                    dve.wait_ge(ring1.sem_full(name), ring1.fills(name, b))
                    q3 = ps[:].rearrange("p (h d) -> p h d", d=DH)
                    nc.vector.tensor_reduce(qmax[:, k % 2, :], q3, axis=AX.X, op=ALU.max).then_inc(qmax_ready, 1)
                    dve.wait_ge(qmax_ready, b.count(T, k + 1))
                    if k >= 2:
                        dve.wait_ge(ring1.sem_full(("qT", k - 2)), ring1.fills(("qT", k - 2), b))
                    nc.vector.tensor_tensor(qw[:, k % 2, :].rearrange("p (h d) -> p h d", d=DH), q3,
                                            qmax[:, k % 2, :].unsqueeze(2).broadcast_to([P, HID // DH, DH]), ALU.subtract)\
                        .then_inc(ring1.sem_free(name), 1)
                if kind == "G":
                    dve.wait_ge(ring1.sem_full(name), ring1.fills(name, b))
                    if k == 0:
                        nc.vector.reciprocal(krec[:], ksum[:]).then_inc(krec_ready, 1)
                        dve.wait_ge(krec_ready, b.count(1, 1))
                    for i in range(2):
                        j = 2 * k + i
                        last = nc.vector.tensor_scalar(G[:, j, :], ps[:, i * D:(i + 1) * D], krec[:, j:j + 1], DH ** -0.5,
                                                       ALU.mult, ALU.mult)
                    last.then_inc(ring1.sem_free(name), 1)
                if kind == "o":
                    dve.wait_ge(ring1.sem_full(name), ring1.fills(name, b))
                    dve.wait_ge(resid_ready, b.count(1, 1))
                    z = x1[:, 2 * k:2 * k + 2, :]
                    nc.vector.tensor_tensor(z, ps[:].rearrange("p (t d) -> p t d", d=D), z, ALU.add)\
                        .then_inc(ring1.sem_free(name), 1)
                    dve.wait_ge(ring1.sem_free(name), ring1.reads(name, b))
                    layernorm_stats(x1, st1, mv1, k, stat1, mean1, b, T, 0)
                    if k == 1:
                        dve.wait_ge(rs1_ready, b.count(1, 1))
                        normalise(x1, mv1, rs1, x1_ready)
                if kind in ("kX", "qX"):
                    n = k + (2 if kind == "qX" else 0)
                    dve.wait_ge(hi_ready, b.count(4, n + 1))
                    if n >= 2 or not b.first:
                        dve.wait_ge(lo_ready, b.count(4, n - 1))
                    nc.vector.scalar_tensor_tensor(rest[:, k, :], ps[:], HD ** -0.5 if kind == "qX" else 1.0, part[:, k, 0, :],
                                                   ALU.mult, ALU.subtract).then_inc(ring1.sem_free(name), 1)

            def sum_q(t, b):
                dve.wait_ge(qexp_ready, b.count(T, t + 1))
                if t >= 2 or not b.first:
                    dve.wait_ge(qn_ready, b.count(T, t - 1))
                nc.vector.tensor_reduce(qsum[:, t % 2, :], qw[:, t % 2, :].rearrange("p (h d) -> p h d", d=DH), axis=AX.X,
                                        op=ALU.add).then_inc(qsum_ready, 1)
                dve.wait_ge(qsum_ready, b.count(T, t + 1))
                nc.vector.reciprocal(qrec[:, t % 2, :], qsum[:, t % 2, :]).then_inc(qrec_ready, 1)

            def stage2(name, b):
                kind, k = name
                ps = ring2.bank(name)
                if kind in ("y", "f4"):
                    dve.wait_ge(ring2.sem_full(name), ring2.fills(name, b))
                    z = x2[:, 2 * k:2 * k + 2, :]
                    if kind == "y":
                        dve.wait_ge(stored, b.count(16, 16))
                        other = x1b[:, b.parity, 2 * k:2 * k + 2, :]
                        dve.wait_ge(x1b_ready, b.count(1, 1))
                    else:
                        other = z
                        dve.wait_ge(resid2_ready, b.count(1, 1))
                    nc.vector.tensor_tensor(z, ps[:].rearrange("p (t d) -> p t d", d=D), other, ALU.add)\
                        .then_inc(ring2.sem_free(name), 1)
                    dve.wait_ge(ring2.sem_free(name), ring2.reads(name, b))
                    base = 0 if kind == "y" else T
                    layernorm_stats(x2, st2, mv2, k, stat2, mean2, b, 2 * T, base)
                    if k == 1:
                        dve.wait_ge(rs2_ready, b.count(2, 1 + base // T))
                        normalise(x2, mv2, rs2, x2_ready)
                if kind == "f2":
                    dve.wait_ge(ring2.sem_free(name), ring2.reads(name, b))
                    dve.wait_ge(hu_ready, b.count(NF, k + 1))
                    nc.vector.scalar_tensor_tensor(hv[:, k % 2, :], hv[:, k % 2, :], 1.0 / GELU_CUBIC, hu[:, k % 2, :],
                                                   ALU.add, ALU.mult).then_inc(hv_ready, 1)
                if name == ("f3", 1):
                    dve.wait_ge(ring2.sem_full(name), ring2.fills(name, b))
                    dve.wait_ge(ring2.sem_free(("f3", 0)), ring2.reads(("f3", 0), b))
                    nc.vector.scalar_tensor_tensor(r2[:], ps[:], 0.5, r2[:], ALU.mult, ALU.add).then_inc(ring2.sem_free(name), 1)

            def stage2_late(name, b):
                kind, k = name
                if kind == "f2":
                    dve.wait_ge(tanh_ready, b.count(NF, k + 1))
                    if k >= 4:
                        dve.wait_ge(ring2.sem_full(("f3", 0)), ring2.fills(("f3", 0), b))
                    nc.vector.scalar_tensor_tensor(h[:, k % 4, :], hv[:, k % 2, :], 1.0, hu[:, k % 2, :], ALU.add, ALU.mult)\
                        .then_inc(h_ready, 1)

            def max_scores(s, i, b):
                g, t = unit_group(s)
                name = ("s", s, i)
                dve.wait_ge(ring_max.sem_full(name), ring_max.fills(name, b))
                nc.vector.tensor_reduce(mx[:, g, i, t:t + 1], ring_max.bank(name)[:], axis=AX.X, op=ALU.max)\
                    .then_inc(ring_max.sem_free(name), 1)

            def split_max(g, b):
                name = ("m", g)
                ps = ring_max.bank(name)[0:4 * T, 0:P]
                dve.wait_ge(ring_max.sem_full(name), ring_max.fills(name, b))
                if g >= 2:
                    dve.wait_ge(maxrow_loaded[g - 2], b.count(48, 48))
                else:
                    if not b.first:
                        dve.wait_ge(maxrow_loaded[g + 2], b.count(48, 0))
                nc.vector.tensor_scalar(mpart[:, g % 2, 0, :], ps, -1.0, None, ALU.mult).then_inc(mhi_ready, 1)
                dve.wait_ge(mhi_ready, b.count(GR, g + 1))
                nc.vector.scalar_tensor_tensor(mrest[:, g % 2, :], ps, -1.0, mpart[:, g % 2, 0, :], ALU.mult, ALU.subtract)\
                    .then_inc(ring_max.sem_free(name), 1)

            def divide_o(g, b):
                dve.wait_ge(o_turned, b.count(GR, g + 1))
                ps = ps_av[:].rearrange("p (t i d) -> p t i d", t=T, i=4)
                nc.vector.reciprocal(orec[:].unsqueeze(3), ps[:, :, :, HD:HD + 1]).then_inc(orec_ready, 1)
                dve.wait_ge(orec_ready, b.count(GR, g + 1))
                if g == 0:
                    for c in range(C):
                        if not b.first:
                            dve.wait_ge(ring2.sem_full(("oT", c)), ring2.fills(("oT", c), b.shifted(-1)))
                nc.vector.tensor_tensor(oN[:, :, 64 * g:64 * (g + 1)].rearrange("p t (i d) -> p t i d", i=4),
                                        ps[:, :, :, 0:HD], orec[:].unsqueeze(3).broadcast_to([P, T, 4, HD]), ALU.mult)\
                    .then_inc(o_ready, 1)

            def slot(s, bx, b1_, b2_):
                ones = STAGE1_AT.get(s, []) if b1_ is not None else []
                for i in range(2):
                    if bx is not None and s < UNITS:
                        max_scores(s, i, bx)
                if bx is not None and s >= EXP_LAG + 5 and (s - EXP_LAG - 5) % 4 == 0:
                    divide_o((s - EXP_LAG - 5) // 4, bx)
                for name in ones[:1]:
                    stage1(name, b1_)
                for i in range(2, 4):
                    if bx is not None and s < UNITS:
                        max_scores(s, i, bx)
                if bx is not None and s % 4 == 0 and 4 <= s <= UNITS:
                    split_max(s // 4 - 1, bx)
                if b2_ is not None and s == 0:
                    divide_o(GR - 1, b2_)
                for name in ones[1:]:
                    stage1(name, b1_)
                if b2_ is not None and s in STAGE2_AT:
                    stage2(STAGE2_AT[s], b2_)
                    stage2_late(STAGE2_AT[s], b2_)

            run(dve, slot)

        @block.gpsimd
        def _(pool):
            nc.gpsimd.memset(ident[:], 0.0).then_inc(const_ready, 1)
            pool.wait_ge(const_ready, 1)
            nc.gpsimd.affine_select(out=ident[:], in_=ident[:], compare_op=ALU.not_equal, fill=1.0, base=0,
                                    pattern=[[-1, P]], channel_multiplier=1).then_inc(diag_ready, 1)
            for dst, src in ((bo_a, a_bo), (bo_c, c_bo), (b2_s, b2)):
                pool.dma_start(dst[:], src.rearrange("(a d) -> a d", a=1).broadcast_to([P, D])).then_inc(rows_loaded, 16)
            pool.wait_ge(rows_loaded, 3 * 16)
            pool.wait_ge(init_ready, 1)

            def add_row(dst, src, row, s_done):
                return nc.gpsimd.tensor_tensor(dst, src, row[:].unsqueeze(1).broadcast_to([P, T, D]), ALU.add).then_inc(s_done, 1)

            def rsqrt(mv, sd, rs, s_mean, s_sd, s_done, b, per, more):
                pool.wait_ge(s_mean, b.count(per * T, more * T))
                pool.sem_inc(pool_alone, 1)
                nc.gpsimd.tensor_scalar(sd[:], mv[:, :, 1], EPS, None, ALU.add).then_inc(s_sd, 1)
                pool.wait_ge(s_sd, b.count(per, more))
                pool.sem_inc(pool_alone, 1)
                nc.gpsimd.tensor_tensor(rs[:], sd[:], minus_half[:], ALU.pow).then_inc(s_done, 1)

            def stage1(name, b):
                kind, k = name
                if name == ("xT", 0):
                    pool.wait_ge(x_loaded, b.count(16, 16))
                    pool.sem_inc(pool_alone, 1)
                    if not b.first:
                        pool.wait_ge(x1b_ready, b.count(1, 0))
                        pool.sem_inc(pool_alone, 1)
                    for c in range(C):
                        if not b.first:
                            pool.wait_ge(ring1.sem_full(("x1T", c)), ring1.fills(("x1T", c), b.shifted(-1)))
                            pool.sem_inc(pool_alone, 1)
                    add_row(x1[:], x_s[:], bo_a, resid_ready)
                if kind in ("kX", "qX"):
                    n = k + (2 if kind == "qX" else 0)
                    pool.wait_ge(ring1.sem_free(name), ring1.reads(name, b))
                    pool.sem_inc(pool_alone, 1)
                    nc.gpsimd.tensor_copy(part[:, k, 1, :], rest[:, k, :]).then_inc(mid_ready, 1)
                    pool.wait_ge(mid_ready, b.count(4, n + 1))
                    pool.sem_inc(pool_alone, 1)
                    nc.gpsimd.tensor_tensor(part[:, k, 2, :], rest[:, k, :], part[:, k, 1, :], ALU.subtract).then_inc(lo_ready, 1)
                if name == ("o", 1):
                    rsqrt(mv1, sd1, rs1, mean1, sd1_ready, rs1_ready, b, 1, 1)
                if name == ("x1T", 0):
                    pool.wait_ge(x1_ready, b.count(T, T))
                    pool.sem_inc(pool_alone, 1)
                    if b.off >= 2:
                        pool.wait_ge(ring2.sem_free(("y", 1)), ring2.reads(("y", 1), b.shifted(-2)))
                        pool.sem_inc(pool_alone, 1)
                    add_row(x1b[:, b.parity, :, :], x1[:], bo_c, x1b_ready)

            def scale_q(t, b):
                pool.wait_ge(qrec_ready, b.count(T, t + 1))
                pool.sem_inc(pool_alone, 1)
                w = qw[:, t % 2, :].rearrange("p (h d) -> p h d", d=DH)
                nc.gpsimd.tensor_tensor(w, w, qrec[:, t % 2, :].unsqueeze(2).broadcast_to([P, HID // DH, DH]), ALU.mult)\
                    .then_inc(qn_ready, 1)

            def split_max(g, b):
                pool.wait_ge(ring_max.sem_free(("m", g)), ring_max.reads(("m", g), b))
                pool.sem_inc(pool_alone, 1)
                nc.gpsimd.tensor_copy(mpart[:, g % 2, 1, :], mrest[:, g % 2, :]).then_inc(mmid_ready, 1)
                pool.wait_ge(mmid_ready, b.count(GR, g + 1))
                pool.sem_inc(pool_alone, 1)
                nc.gpsimd.tensor_tensor(mpart[:, g % 2, 2, :], mrest[:, g % 2, :], mpart[:, g % 2, 1, :], ALU.subtract)\
                    .then_inc(mlo_ready, 1)

            def stage2(name, b):
                if name == ("y", 1):
                    rsqrt(mv2, sd2, rs2, mean2, sd2_ready, rs2_ready, b, 2, 1)
                if name == ("f4", 1):
                    rsqrt(mv2, sd2, rs2, mean2, sd2_ready, rs2_ready, b, 2, 2)
                if name == ("x2T", 1):
                    for c in range(C):
                        pool.wait_ge(ring2.sem_full(("x2T", c)), ring2.fills(("x2T", c), b))
                        pool.sem_inc(pool_alone, 1)
                    pool.wait_ge(x2_ready, b.count(2 * T, T))
                    pool.sem_inc(pool_alone, 1)
                    add_row(x2[:], x2[:], b2_s, resid2_ready)

            def slot(s, bx, b1_, b2_):
                ones = STAGE1_AT.get(s, []) if b1_ is not None else []
                for name in ones[:1]:
                    stage1(name, b1_)
                    if name in Q_SUM_AT:
                        scale_q(Q_SUM_AT[name], b1_)
                if bx is not None and s % 4 == 0 and 4 <= s <= UNITS:
                    split_max(s // 4 - 1, bx)
                for name in ones[1:]:
                    stage1(name, b1_)
                    if name in Q_SUM_AT:
                        scale_q(Q_SUM_AT[name], b1_)
                if b2_ is not None and s in STAGE2_AT:
                    stage2(STAGE2_AT[s], b2_)

            run(pool, slot)


_INS = ["x", "ctx_768", "L0_attn_Wq", "L0_attn_Wk", "L0_attn_Wv", "L0_attn_Wo", "L0_attn_bo", "L0_xattn_Wq", "L0_xattn_Wk",
        "L0_xattn_Wv", "L0_xattn_Wo", "L0_xattn_bo", "L0_ffn_U1", "L0_ffn_V1", "L0_ffn_b1", "L0_ffn_U2", "L0_ffn_V2", "L0_ffn_b2"]


def kernel(**inputs):
    import numpy as np
    import concourse.bacc as bacc
    from concourse.bass_utils import run_bass_kernel_spmd

    nc = bacc.Bacc("TRN2", target_bir_lowering=False, num_devices=1)
    arrays, args = {}, []
    for name in _INS:
        a = np.ascontiguousarray(inputs[name])
        arrays[f"in_{name}"] = a
        args.append(nc.dram_tensor(f"in_{name}", a.shape, mybir.dt.from_np(a.dtype), kind="ExternalInput").ap())
    out = nc.dram_tensor("out_0", inputs["x"].shape, F32, kind="ExternalOutput").ap()
    decoder_layer(nc, *args, out)
    r = run_bass_kernel_spmd(nc, [arrays], core_ids=[0])
    return r.results[0]["out_0"]
```

```python
from contextlib import ExitStack

import concourse.bass as bass
from concourse import mybir

F32 = mybir.dt.float32
F32R = mybir.dt.float32r
BF16 = mybir.dt.bfloat16
ALU = mybir.AluOpType
ACT = mybir.ActivationFunctionType
AX = mybir.AxisListType

P = 128
EPS = 1e-5
GELU_CUBIC = 0.044715
GELU_SCALE = 0.7978845608028654

STAGE1_AT = {
    1: [("cT", 0), ("cT", 1)],
    2: [("kX", 0), ("kX", 1)],
    3: [("vX", 0), ("vX", 1)],
    4: [("xT", 0), ("xT", 1)],
    5: [("k", 0), ("q", 0)],
    6: [("k", 1), ("q", 1)],
    7: [("k", 2), ("qT", 0)],
    8: [("k", 3), ("q", 2)],
    9: [("ek", 0), ("qT", 1)],
    10: [("ek", 1), ("q", 3)],
    11: [("ek", 2), ("qT", 2)],
    12: [("ek", 3), ("xTk", 0)],
    13: [("xTk", 1), ("qT", 3), ("ctx", 0)],
    14: [("G", 0), ("G", 1)],
    15: [("o", 0), ("o", 1)],
    17: [("x1T", 0), ("x1T", 1)],
    18: [("qX", 0), ("qX", 1)],
}
Q_SUM_AT = {("q", 1): 0, ("qT", 0): 1, ("qT", 1): 2, ("qT", 2): 3}
STAGE2_AT = {
    1: [("oT", 0), ("oT", 1)], 2: [("y", 0)], 3: [("y", 1)], 5: [("x2T", 0)], 6: [("x2T", 1)], 7: [("f1", 0)],
    8: [("f2", 0)], 9: [("f2", 1)], 10: [("f2", 2)], 11: [("f2", 3)], 12: [("f2", 4)],
    13: [("f3", 0), ("f2", 5)], 14: [("f2", 6)], 15: [("f2", 7)], 17: [("f3", 1)], 18: [("f4", 0)], 19: [("f4", 1)],
}
NORM1_AT, NORM2_AT, NORM3_AT = 16, 4, 20
SLOTS = 22
MAX_LAG = 1
EXP_LAG = 6
TURN_LAG = EXP_LAG + 5


class Batch:

    def __init__(self, off, loop=None):
        self.off, self.loop = off, loop

    def shifted(self, by):
        return Batch(self.off + by, self.loop)

    @property
    def parity(self):
        return self.off % 2

    @property
    def first(self):
        return self.loop is None and self.off == 0

    def index(self):
        return self.off if self.loop is None else self.loop * 2 + self.off

    def count(self, per_batch, more):
        if self.loop is None:
            return self.off * per_batch + more
        return self.loop * (2 * per_batch) + (self.off * per_batch + more)


class Ring:

    def __init__(self, order, banks, full, free):
        self.place = {name: (n % len(banks), n // len(banks)) for n, name in enumerate(order)}
        self.uses = [len(order[i::len(banks)]) for i in range(len(banks))]
        self.banks, self.full, self.free = banks, full, free

    def bank(self, name):
        return self.banks[self.place[name][0]]

    def sem_full(self, name):
        return self.full[self.place[name][0]]

    def sem_free(self, name):
        return self.free[self.place[name][0]]

    def fills(self, name, batch):
        i, k = self.place[name]
        return batch.count(self.uses[i], k + 1)

    def frees(self, name, batch):
        i, k = self.place[name]
        return batch.count(self.uses[i], k + 1)

    def reads(self, name, batch):
        i, k = self.place[name]
        return batch.count(self.uses[i], k + 2)

    def all_read(self, names, batch, then=None):
        need = {}
        for name in names:
            i, k = self.place[name]
            need[i] = max(need.get(i, 0), k + 2)
        if then is not None:
            i, k = self.place[then]
            need[i] = max(need.get(i, 0), k + 1)
        return [(self.free[i], batch.count(self.uses[i], k)) for i, k in need.items()]


def decoder_layer(nc, x, ctx_768, a_wq, a_wk, a_wv, a_wo, a_bo, c_wq, c_wk, c_wv, c_wo, c_bo,
                  u1, v1, b1, u2, v2, b2, out):
    B, N, D = x.shape
    M, CD = ctx_768.shape[1:]
    HID = a_wq.shape[1]
    DH = 64
    HEADS, HD = 16, D // 16
    R, F = v1.shape
    T = N // P
    C = D // P
    J = HID // P
    GR = HEADS // 4
    NF = F // P
    UNITS = GR * T
    PARTS = 3 * HD
    PROD = 6 * HD
    assert (N, M, D, HID, R, T, C, J) == (512, 512, 256, 512, 64, 4, 2, 4) and B % 2 == 0 and CD == 192

    x_v = x.rearrange("b (p t) d -> b p t d", t=T)
    c_v = ctx_768.rearrange("b (p t) d -> b p t d", t=T)
    out_v = out.rearrange("b (p t) d -> b p t d", t=T)
    q_parts = nc.dram_tensor("q_parts", [HEADS, PARTS, N], BF16, kind="Internal").ap()
    k_parts = nc.dram_tensor("k_parts", [HEADS, PARTS, M], BF16, kind="Internal").ap()

    es = ExitStack()
    with es:
        def sb(name, shape, dt=F32):
            return es.enter_context(nc.sbuf_tensor(name, shape, dt))

        def sem(name):
            return es.enter_context(nc.semaphore(name))

        def sems(name, n):
            return [sem(f"{name}{i}") for i in range(n)]

        wq_a, wk_a, wv_a = sb("wq_a", [P, C, HID]), sb("wk_a", [P, C, HID]), sb("wv_a", [P, C, HID])
        wo_a = sb("wo_a", [P, J, D])
        wq_c, wk_c, wv_c, wo_c = (sb(n, [P, C, D]) for n in ("wq_c", "wk_c", "wv_c", "wo_c"))
        u1_s = sb("u1_s", [P, C, 2, R])
        v1_hi, v1_lo = sb("v1_hi", [2 * R, F], F32R), sb("v1_lo", [2 * R, F], F32R)
        u2_s, v2_s = sb("u2_s", [P, NF, R]), sb("v2_s", [2 * R, D])
        b1_s = sb("b1_s", [P, NF])
        bo_a, bo_c, b2_s = sb("bo_a", [P, D]), sb("bo_c", [P, D]), sb("b2_s", [P, D])
        ident = sb("ident", [P, P])
        minus_half = sb("minus_half", [P, T])

        x_s = sb("x_s", [P, T, D])
        c_s = sb("c_s", [P, T, CD])
        tokT = sb("tokT", [P, C, N])
        ekT = sb("ekT", [P, J, N])
        ek = sb("ek", [P, T, HID])
        kneg, ksum, krec = sb("kneg", [P, J]), sb("ksum", [P, J]), sb("krec", [P, J])
        xTk = sb("xTk", [P, C, HID])
        ctxT = sb("ctxT", [P, J, P])
        G = sb("G", [P, J, D])
        qw = sb("qw", [P, 2, HID])
        qmax, qsum, qrec = (sb(n, [P, 2, HID // DH]) for n in ("qmax", "qsum", "qrec"))
        qT = sb("qT", [P, J, N])
        x1 = sb("x1", [P, T, D])
        st1, mv1, sd1, rs1 = sb("st1", [P, T, 6]), sb("mv1", [P, T, 2]), sb("sd1", [P, T]), sb("rs1", [P, T])
        part = sb("part", [P, 2, 3, N], BF16)
        rest = sb("rest", [P, 2, N])
        x1b = sb("x1b", [P, 2, T, D])
        vX = sb("vX", [P, 2, T, HEADS, HD + 1])
        QS = sb("QS", [P, HEADS, N], BF16)
        KS = sb("KS", [P, HEADS, M], BF16)
        mx = sb("mx", [P, GR, 4, T])
        mpart = sb("mpart", [4 * T, 2, 3, P], BF16)
        mrest = sb("mrest", [4 * T, 2, P])
        probs = sb("probs", [P, 8, N])
        oTs = sb("oTs", [P, N])
        orec = sb("orec", [P, T, 4])
        oN = sb("oN", [P, T, D])
        oT = sb("oT", [P, C, N])
        x2 = sb("x2", [P, T, D])
        st2, mv2, sd2, rs2 = sb("st2", [P, T, 6]), sb("mv2", [P, T, 2]), sb("sd2", [P, T]), sb("rs2", [P, T])
        pT = sb("pT", [2 * R, N], F32R)
        hu, hv = sb("hu", [P, 2, N]), sb("hv", [P, 2, N])
        h = sb("h", [P, 4, N])
        r2 = sb("r2", [2 * R, N])
        v1_raw = h[:, 0:2, :].rearrange("p a n -> p (a n)")

        def banks(name, n):
            return [es.enter_context(nc.psum_tensor(f"{name}{i}", [P, 512], F32)) for i in range(n)]

        order1 = [name for s in sorted(STAGE1_AT) for name in STAGE1_AT[s]]
        order2 = [name for s in sorted(STAGE2_AT) for name in STAGE2_AT[s]]
        order_max = []
        for u in range(4 * GR + 1):
            for i in range(4):
                order_max += [("s", u, i)] if u < 4 * GR else []
                order_max += [("m", u // 4 - 1)] if u % 4 == 0 and u and i == 0 else []
        order_exp = [("e", u, i) for u in range(UNITS) for i in range(4)]
        ring1 = Ring(order1, banks("ps_one", 2), sems("one_full", 2), sems("one_read", 2))
        ring2 = Ring(order2, banks("ps_two", 1), sems("two_full", 1), sems("two_read", 1))
        ring_max = Ring(order_max, banks("ps_max", 2), sems("max_full", 2), sems("max_read", 2))
        ring_exp = Ring(order_exp, banks("ps_exp", 2), sems("exp_full", 2), sems("exp_read", 2))
        ps_av = banks("ps_av", 1)[0]

        wkc_loaded, wvc_loaded, wka_loaded, wqa_loaded, wva_loaded, woa_loaded, wqc_loaded, woc_loaded, ffn_loaded = (
            sem(n) for n in ("wkc_loaded", "wvc_loaded", "wka_loaded", "wqa_loaded", "wva_loaded", "woa_loaded", "wqc_loaded",
                             "woc_loaded", "ffn_loaded"))
        v1_loaded, v1_hi_ready, v1_ready = sem("v1_loaded"), sem("v1_hi_ready"), sem("v1_ready")
        p_ready = sem("p_ready")
        ones_ready, const_ready, diag_ready, init_ready = sem("ones_ready"), sem("const_ready"), sem("diag_ready"), sem("init_ready")
        rows_loaded = sem("rows_loaded")
        sp_alone, pool_alone, dve_alone, pe_alone = (sem(n) for n in ("sp_alone", "pool_alone", "dve_alone", "pe_alone"))
        x_loaded, c_loaded, stored = sem("x_loaded"), sem("c_loaded"), sem("stored")
        parts_written = sems("parts_written", 2)
        stack_loaded = sems("stack_loaded", GR)
        maxrow_loaded = sems("maxrow_loaded", GR)
        kneg_ready, krec_ready = sem("kneg_ready"), sem("krec_ready")
        qmax_ready, qexp_ready, qsum_ready, qrec_ready, qn_ready = (sem(n) for n in (
            "qmax_ready", "qexp_ready", "qsum_ready", "qrec_ready", "qn_ready"))
        resid_ready = sem("resid_ready")
        stat1, mean1, sd1_ready, rs1_ready, x1_ready, x1b_ready = (sem(n) for n in (
            "stat1", "mean1", "sd1_ready", "rs1_ready", "x1_ready", "x1b_ready"))
        hi_ready, mid_ready, lo_ready = sem("hi_ready"), sem("mid_ready"), sem("lo_ready")
        mhi_ready, mrest_ready, mmid_ready, mlo_ready = (sem(n) for n in (
            "mhi_ready", "mrest_ready", "mmid_ready", "mlo_ready"))
        av_done = sem("av_done")
        o_copied, o_turned, orec_ready, o_ready = (sem(n) for n in ("o_copied", "o_turned", "orec_ready", "o_ready"))
        resid2_ready = sem("resid2_ready")
        stat2, mean2, sd2_ready, rs2_ready, x2_ready = (sem(n) for n in (
            "stat2", "mean2", "sd2_ready", "rs2_ready", "x2_ready"))
        hu_ready, hv_ready, tanh_ready, h_ready = sem("hu_ready"), sem("hv_ready"), sem("tanh_ready"), sem("h_ready")

        N_FFN = 6

        def unit_group(u):
            return u // T, u % T

        block = es.enter_context(nc.Block())

        def run(engine, slot):
            for s in range(SLOTS):
                slot(s, None, Batch(0), None)
            for s in range(SLOTS):
                slot(s, Batch(0), Batch(1), None)
            with engine.Fori(0, (B - 2) // 2) as i:
                for off in (1, 2):
                    b = Batch(off, i)
                    for s in range(SLOTS):
                        slot(s, b, b.shifted(1), b.shifted(-1))
            for s in range(SLOTS):
                slot(s, Batch(B - 1), None, Batch(B - 2))
            for s in range(SLOTS):
                slot(s, None, None, Batch(B - 1))

        @block.sync
        def _(sp):
            sp.dma_start(c_s[:], c_v[0]).then_inc(c_loaded, 16)
            for dst, src, loaded in ((wk_c, c_wk, wkc_loaded), (wv_c, c_wv, wvc_loaded)):
                sp.dma_start(dst[:, 0, :], src[0:P, :]).then_inc(loaded, 16)
                sp.dma_start(dst[0:CD - P, 1, :], src[P:CD, :]).then_inc(loaded, 16)
            sp.dma_start(x_s[:], x_v[0]).then_inc(x_loaded, 16)
            for dst, src, loaded in ((wk_a, a_wk, wka_loaded), (wq_a, a_wq, wqa_loaded), (wv_a, a_wv, wva_loaded),
                                     (wo_a, a_wo, woa_loaded), (wq_c, c_wq, wqc_loaded), (wo_c, c_wo, woc_loaded),
                                     (u1_s[:, :, 0, :], u1, ffn_loaded), (u1_s[:, :, 1, :], u1, ffn_loaded)):
                sp.dma_start(dst if src is u1 else dst[:], src.rearrange("(c p) n -> p c n", p=P)).then_inc(loaded, 16)
            for half in range(2):
                sp.dma_start(v1_raw[half * R:(half + 1) * R, :], v1).then_inc(v1_loaded, 16)
            sp.dma_start(u2_s[:], u2.rearrange("(p f) r -> p f r", p=P)).then_inc(ffn_loaded, 16)
            for half in range(2):
                sp.dma_start(v2_s[half * R:(half + 1) * R, :], v2).then_inc(ffn_loaded, 16)
            sp.dma_start(b1_s[:], b1.rearrange("(p f) -> p f", p=P)).then_inc(ffn_loaded, 16)

            def stack_in(g, b):
                sp.wait_ge(parts_written[g // 2], b.count(96, 96))
                sp.sem_inc(sp_alone, 1)
                if not b.first:
                    for i in (2, 3):
                        name = ("e", 4 * g + 3, i)
                        sp.wait_ge(ring_exp.sem_full(name), ring_exp.fills(name, b.shifted(-1)))
                        sp.sem_inc(sp_alone, 1)
                hs = slice(4 * g, 4 * g + 4)
                for dst, src, first in ((QS, q_parts, 0), (KS, k_parts, 1)):
                    for row, rows in ((0, 3), (3, 2), (5, 1)):
                        at = (3 - rows) * HD if first else 0
                        sp.dma_start(dst[row * HD:(row + rows) * HD, hs, :],
                                     src[hs, at:at + rows * HD, :].rearrange("h r n -> r h n")).then_inc(stack_loaded[g], 16)

            def parts_out(c, which, b):
                k = 2 * which + c
                sp.wait_ge(lo_ready, b.count(4, k + 1))
                sp.sem_inc(sp_alone, 1)
                if which == 0:
                    for g in range(GR):
                        if not b.first:
                            sp.wait_ge(stack_loaded[g], b.count(96, 0))
                            sp.sem_inc(sp_alone, 1)
                dst = (k_parts, q_parts)[which]
                for i in range(3):
                    at = (i if which else 2 - i) * HD
                    sp.dma_start(dst[8 * c:8 * c + 8, at:at + HD, :], part[:, c, i, :]).then_inc(parts_written[c], 16)

            def slot(s, bx, b1_, b2_):
                if b1_ is not None and s == 0 and not b1_.first:
                    sp.wait_ge(ring1.sem_full(("cT", 1)), ring1.fills(("cT", 1), b1_.shifted(-1)))
                    sp.sem_inc(sp_alone, 1)
                    sp.dma_start(c_s[:], c_v[b1_.index()]).then_inc(c_loaded, 16)
                    sp.wait_ge(ring1.sem_full(("xTk", 0)), ring1.fills(("xTk", 0), b1_.shifted(-1)))
                    sp.sem_inc(sp_alone, 1)
                    sp.wait_ge(ring1.sem_full(("xTk", 1)), ring1.fills(("xTk", 1), b1_.shifted(-1)))
                    sp.sem_inc(sp_alone, 1)
                    sp.wait_ge(resid_ready, b1_.count(1, 0))
                    sp.sem_inc(sp_alone, 1)
                    sp.dma_start(x_s[:], x_v[b1_.index()]).then_inc(x_loaded, 16)
                if bx is not None and 0 <= s < GR - 1:
                    stack_in(s + 1, bx)
                if b1_ is not None:
                    for kind, c in STAGE1_AT.get(s, []):
                        if kind in ("kX", "qX"):
                            parts_out(c, 0 if kind == "kX" else 1, b1_)
                g, rest_of = divmod(s - MAX_LAG - 4, 4)
                if bx is not None and rest_of == 0 and 0 <= g < GR:
                    sp.wait_ge(mlo_ready, bx.count(GR, g + 1))
                    sp.sem_inc(sp_alone, 1)
                    for i in range(3):
                        sp.dma_start(QS[PROD + i:PROD + i + 1, 4 * g:4 * g + 4, :].rearrange("a h (t n) -> a (h t) n", n=P),
                                     mpart[:, g % 2, i, :]).then_inc(maxrow_loaded[g], 16)
                if b2_ is not None and s == NORM3_AT:
                    sp.wait_ge(x2_ready, b2_.count(8, 8))
                    sp.sem_inc(sp_alone, 1)
                    sp.dma_start(out_v[b2_.index()], x2[:]).then_inc(stored, 16)
                if b1_ is not None and s == SLOTS - 1:
                    stack_in(0, b1_)

            run(sp, slot)
            sp.wait_ge(stored, 16 * (B + 1))

        @block.tensor
        def _(pe):
            pe.wait_ge(diag_ready, 1)
            pe.wait_ge(init_ready, 1)

            def mm(dst, lhsT, rhs, start, stop, **kw):
                return nc.tensor.matmul(dst, lhsT, rhs, start=start, stop=stop, **kw)

            def transpose(dst, src):
                return nc.tensor.transpose(dst, src, ident[0:src.shape[0], 0:src.shape[0]])

            def tile(t):
                return slice(t * P, (t + 1) * P)

            needs1 = {"kX": [("cT", 0), ("cT", 1)], "vX": [("cT", 0), ("cT", 1)], "k": [("xT", 0), ("xT", 1)],
                      "q": [("xT", 0), ("xT", 1)], "ek": [("k", j) for j in range(J)], "xTk": [("ek", t) for t in range(T)],
                      "ctx": [("xTk", c) for c in range(C)], "G": [("ctx", 0)],
                      "o": [("G", 0), ("G", 1)] + [("qT", t) for t in range(T)], "qX": [("x1T", 0), ("x1T", 1)]}
            needs2 = {"y": [("oT", 0), ("oT", 1)], "f1": [("x2T", 0), ("x2T", 1)], "f2": [("f1", 0)], "f4": [("f3", 1)]}

            weights1 = {("kX", 0): wkc_loaded, ("vX", 0): wvc_loaded, ("k", 0): wka_loaded, ("q", 0): wqa_loaded,
                        ("ctx", 0): wva_loaded, ("G", 0): woa_loaded, ("qX", 0): wqc_loaded}

            def stage1(name, b):
                kind, k = name
                ps = ring1.bank(name)
                if name == ("cT", 0):
                    pe.wait_ge(c_loaded, b.count(16, 16))
                if name == ("xT", 0):
                    pe.wait_ge(x_loaded, b.count(16, 16))
                if b.first and name in weights1:
                    pe.wait_ge(weights1[name], 32 if name in (("kX", 0), ("vX", 0)) else 16)
                if kind == "qT":
                    pe.wait_ge(qn_ready, b.count(T, k + 1))
                if kind == "x1T":
                    pe.wait_ge(x1_ready, b.count(T, T))
                for read, count in ring1.all_read(needs1.get(kind, []), b, then=name):
                    pe.wait_ge(read, count)
                if name == ("cT", 1):
                    pe.sem_inc(pe_alone, 1)
                if kind == "cT":
                    rows = P if k == 0 else CD - P
                    for t in range(T):
                        last = transpose(ps[0:rows, tile(t)], c_s[:, t, k * P:k * P + rows])
                if kind in ("kX", "qX"):
                    w = wk_c if kind == "kX" else wq_c
                    for c in range(2):
                        rows = CD - P if kind == "kX" and c == 1 else P
                        last = mm(ps[:], w[0:rows, c, k * P:(k + 1) * P], tokT[0:rows, c, :], c == 0, c == 1)
                if kind == "vX":
                    for i in range(2):
                        for c in range(2):
                            rows = CD - P if c == 1 else P
                            last = mm(ps[:, i * D:(i + 1) * D], tokT[0:rows, c, tile(2 * k + i)], wv_c[0:rows, c, :],
                                      c == 0, c == 1)
                if kind in ("xT", "x1T"):
                    src = x_s if kind == "xT" else x1
                    for t in range(T):
                        last = transpose(ps[:, tile(t)], src[:, t, k * P:(k + 1) * P])
                if kind == "k":
                    for c in range(C):
                        last = mm(ps[:], wk_a[:, c, tile(k)], tokT[:, c, :], c == 0, c == C - 1)
                if kind == "q":
                    for c in range(C):
                        last = mm(ps[:], tokT[:, c, tile(k)], wq_a[:, c, :], c == 0, c == C - 1)
                if kind == "ek":
                    for j in range(J):
                        last = transpose(ps[:, tile(j)], ekT[:, j, tile(k)])
                if kind == "xTk":
                    for t in range(T):
                        last = mm(ps[:], x_s[:, t, k * P:(k + 1) * P], ek[:, t, :], t == 0, t == T - 1)
                if kind == "ctx":
                    for j in range(J):
                        for c in range(C):
                            last = mm(ps[:, tile(j)], wv_a[:, c, tile(j)], xTk[:, c, tile(j)], c == 0, c == C - 1)
                if kind == "G":
                    for i in range(2):
                        last = mm(ps[:, i * D:(i + 1) * D], ctxT[:, 2 * k + i, :], wo_a[:, 2 * k + i, :], True, True)
                if kind == "qT":
                    for j in range(J):
                        last = transpose(ps[:, tile(j)], qw[:, k % 2, tile(j)])
                if kind == "o":
                    for i in range(2):
                        for j in range(J):
                            last = mm(ps[:, i * D:(i + 1) * D], qT[:, j, tile(2 * k + i)], G[:, j, :], j == 0, j == J - 1)
                last.then_inc(ring1.sem_full(name), 1)

            def stage2(name, b):
                kind, k = name
                ps = ring2.bank(name)
                if b.first and name == ("y", 0):
                    pe.wait_ge(woc_loaded, 16)
                if b.first and name == ("f1", 0):
                    pe.wait_ge(ffn_loaded, 16 * N_FFN)
                    pe.wait_ge(v1_ready, 1)
                if kind == "oT":
                    pe.wait_ge(o_ready, b.count(GR, GR))
                if kind == "x2T":
                    pe.wait_ge(x2_ready, b.count(2 * T, T))
                if kind == "f3":
                    pe.wait_ge(h_ready, b.count(NF, 4 * k + 4))
                for read, count in ring2.all_read(needs2.get(kind, []), b, then=name):
                    pe.wait_ge(read, count)
                if kind in ("oT", "x2T"):
                    src = oN if kind == "oT" else x2
                    for t in range(T):
                        last = transpose(ps[:, tile(t)], src[:, t, k * P:(k + 1) * P])
                if kind == "y":
                    for i in range(2):
                        for c in range(C):
                            last = mm(ps[:, i * D:(i + 1) * D], oT[:, c, tile(2 * k + i)], wo_c[:, c, :], c == 0, c == C - 1)
                if kind == "f1":
                    for c in range(C):
                        last = mm(ps[:], u1_s[:, c, :, :].rearrange("p a r -> p (a r)"), oT[:, c, :], c == 0, c == C - 1)
                if kind == "f2":
                    mm(ps[:], v1_lo[:, k::NF], pT[:], True, False)
                    last = mm(ps[:], v1_hi[:, k::NF], pT[:], False, True)
                if kind == "f3":
                    for i in range(4):
                        half = i % 2
                        last = mm(ps[half * R:(half + 1) * R, :], u2_s[:, 4 * k + i, :], h[:, i, :], i < 2, i >= 2)
                if kind == "f4":
                    for i in range(2):
                        last = mm(ps[:, i * D:(i + 1) * D], r2[:, tile(2 * k + i)], v2_s[:], True, True)
                last.then_inc(ring2.sem_full(name), 1)

            def scores_for_max(s, i, b):
                g, t = unit_group(s)
                name, head = ("s", s, i), 4 * g + i
                if i == 0 and t == 0:
                    pe.wait_ge(stack_loaded[g], b.count(96, 96))
                pe.wait_ge(ring_max.sem_free(name), ring_max.frees(name, b))
                mm(ring_max.bank(name)[:], QS[0:PROD, head, tile(t)], KS[0:PROD, head, :], True, True)\
                    .then_inc(ring_max.sem_full(name), 1)

            def turn_max(g, b):
                name = ("m", g)
                for read, count in ring_max.all_read([("s", 4 * g + 3, 2), ("s", 4 * g + 3, 3)], b, then=name):
                    pe.wait_ge(read, count)
                transpose(ring_max.bank(name)[0:4 * T, 0:P], mx[:, g, :, :].rearrange("p h t -> p (h t)"))\
                    .then_inc(ring_max.sem_full(name), 1)

            def scores_for_exp(u, i, b):
                g, mc = unit_group(u)
                name, head = ("e", u, i), 4 * g + i
                if u == 0 and i == 0 and b.first:
                    pe.wait_ge(ones_ready, 1)
                if i == 0 and mc == 0:
                    pe.wait_ge(maxrow_loaded[g], b.count(48, 48))
                pe.wait_ge(ring_exp.sem_free(name), ring_exp.frees(name, b))
                mm(ring_exp.bank(name)[:], KS[0:PROD + 3, head, tile(mc)], QS[0:PROD + 3, head, :], True, True)\
                    .then_inc(ring_exp.sem_full(name), 1)

            def probs_times_v(u, b):
                g, mc = unit_group(u)
                if mc == 0:
                    if g or not b.first:
                        pe.wait_ge(o_ready, b.count(GR, g))
                    if g == 0:
                        for read, count in ring1.all_read([("vX", 0), ("vX", 1)], b):
                            pe.wait_ge(read, count)
                for read, count in ring_exp.all_read([("e", u, i) for i in range(4)], b):
                    pe.wait_ge(read, count)
                for i in range(4):
                    last = mm(ps_av[32 * i:32 * i + HD + 1, :], vX[:, b.parity, mc, 4 * g + i, :],
                              probs[:, 4 * (u % 2) + i, :], mc == 0, mc == T - 1, tile_position=(0, 32 * i))
                last.then_inc(av_done, 1)

            def turn_o(g, b):
                pe.wait_ge(o_copied, b.count(GR, g + 1))
                for t in range(T):
                    last = transpose(ps_av[:, tile(t)], oTs[:, tile(t)])
                last.then_inc(o_turned, 1)

            def slot(s, bx, b1_, b2_):
                ones = STAGE1_AT.get(s, []) if b1_ is not None else []
                twos = STAGE2_AT.get(s, []) if b2_ is not None else []
                um, ue = s - MAX_LAG, s - EXP_LAG
                if b2_ is not None and s == 0:
                    probs_times_v(UNITS - 1, b2_)
                for i in range(4):
                    if bx is not None and 0 <= um < UNITS:
                        scores_for_max(um, i, bx)
                    if i == 0 and bx is not None and um % 4 == 0 and 4 <= um <= UNITS:
                        turn_max(um // 4 - 1, bx)
                    if bx is not None and 0 <= ue < UNITS:
                        scores_for_exp(ue, i, bx)
                    if i == 0:
                        for name in ones[:1]:
                            stage1(name, b1_)
                    if i == 1:
                        if bx is not None and s >= TURN_LAG and (s - TURN_LAG) % 4 == 0:
                            turn_o((s - TURN_LAG) // 4, bx)
                        if b2_ is not None and s == 0:
                            turn_o(GR - 1, b2_)
                        for name in ones[1:]:
                            stage1(name, b1_)
                    if i == 2:
                        for name in twos[:1]:
                            stage2(name, b2_)
                for name in twos[1:]:
                    stage2(name, b2_)
                if bx is not None and 1 <= ue <= UNITS - 1:
                    probs_times_v(ue - 1, bx)

            run(pe, slot)

        @block.scalar
        def _(act):
            def stage1(name, b):
                kind, k = name
                ps = ring1.bank(name)
                if kind in ("G", "o", "q", "cT_"):
                    return
                act.wait_ge(ring1.sem_full(name), ring1.fills(name, b))
                if kind in ("cT", "xT", "x1T"):
                    rows = CD - P if name == ("cT", 1) else P
                    nc.scalar.activation(tokT[0:rows, k, :], ps[0:rows, :], ACT.Copy).then_inc(ring1.sem_free(name), 1)
                if kind in ("kX", "qX"):
                    n = k + (2 if kind == "qX" else 0)
                    if n >= 2:
                        act.wait_ge(parts_written[k], b.count(96, 48))
                    else:
                        if not b.first:
                            act.wait_ge(parts_written[k], b.count(96, 0))
                    nc.scalar.activation(part[:, k, 0, :], ps[:], ACT.Copy, scale=HD ** -0.5 if kind == "qX" else 1.0)\
                        .then_inc(hi_ready, 1)
                if kind == "vX":
                    nc.scalar.activation(vX[:, b.parity, 2 * k:2 * k + 2, :, 0:HD],
                                         ps[:].rearrange("p (t h d) -> p t h d", t=2, h=HEADS), ACT.Copy)\
                        .then_inc(ring1.sem_free(name), 1)
                if kind == "k":
                    act.wait_ge(kneg_ready, b.count(J, k + 1))
                    nc.scalar.activation(ekT[:, k, :], ps[:], ACT.Exp, bias=kneg[:, k:k + 1], accum_out=ksum[:, k:k + 1])\
                        .then_inc(ring1.sem_free(name), 1)
                if kind in ("ek", "xTk"):
                    dst = ek if kind == "ek" else xTk
                    nc.scalar.activation(dst[:, k, :], ps[:], ACT.Copy).then_inc(ring1.sem_free(name), 1)
                if kind == "ctx":
                    for i in range(2):
                        at = slice(i * DH, (i + 1) * DH)
                        last = nc.scalar.activation(ctxT[at, :, at], ps[at, :].rearrange("p (j d) -> p j d", d=P)[:, :, at],
                                                    ACT.Copy)
                    last.then_inc(ring1.sem_free(name), 1)
                if kind == "qT":
                    nc.scalar.activation(qT[:, :, k * P:(k + 1) * P], ps[:].rearrange("p (j n) -> p j n", n=P), ACT.Copy)\
                        .then_inc(ring1.sem_free(name), 1)

            def exp_q(t, b):
                act.wait_ge(ring1.sem_free(("q", t)), ring1.reads(("q", t), b))
                nc.scalar.activation(qw[:, t % 2, :], qw[:, t % 2, :], ACT.Exp).then_inc(qexp_ready, 1)

            def stage2(name, b):
                kind, k = name
                ps = ring2.bank(name)
                if kind in ("y", "f4") or name == ("f3", 1):
                    return
                act.wait_ge(ring2.sem_full(name), ring2.fills(name, b))
                free = ring2.sem_free(name)
                if kind in ("oT", "x2T"):
                    nc.scalar.activation(oT[:, k, :], ps[:], ACT.Copy).then_inc(free, 1)
                if kind == "f1":
                    nc.scalar.activation(pT[:], ps[:], ACT.Copy).then_inc(p_ready, 1)
                if kind == "f2":
                    if k >= 2:
                        act.wait_ge(h_ready, b.count(NF, k - 1))
                    if b.first and k == 0:
                        act.wait_ge(ffn_loaded, 16 * N_FFN)
                    nc.scalar.activation(hu[:, k % 2, :], ps[:], ACT.Identity, bias=b1_s[:, k:k + 1]).then_inc(hu_ready, 1)
                    nc.scalar.activation(hv[:, k % 2, :], ps[:], ACT.Square, bias=b1_s[:, k:k + 1]).then_inc(free, 1)
                if kind == "f3":
                    nc.scalar.activation(r2[:], ps[:], ACT.Copy, scale=0.5).then_inc(free, 1)

            def tanh_h(name, b):
                kind, k = name
                if kind == "f2":
                    act.wait_ge(hv_ready, b.count(NF, k + 1))
                    nc.scalar.activation(hv[:, k % 2, :], hv[:, k % 2, :], ACT.Tanh, scale=GELU_SCALE * GELU_CUBIC)\
                        .then_inc(tanh_ready, 1)

            def exp_scores(u, i, b):
                name = ("e", u, i)
                if u >= 2 or not b.first:
                    act.wait_ge(av_done, b.count(UNITS, u - 1))
                act.wait_ge(ring_exp.sem_full(name), ring_exp.fills(name, b))
                nc.scalar.activation(probs[:, 4 * (u % 2) + i, :], ring_exp.bank(name)[:], ACT.Exp)\
                    .then_inc(ring_exp.sem_free(name), 1)

            def copy_o(g, b):
                act.wait_ge(av_done, b.count(UNITS, 4 * (g + 1)))
                nc.scalar.activation(oTs[:], ps_av[:], ACT.Copy).then_inc(o_copied, 1)

            act.wait_ge(init_ready, 1)

            def slot(s, bx, b1_, b2_):
                ones = STAGE1_AT.get(s, []) if b1_ is not None else []
                twos = STAGE2_AT.get(s, []) if b2_ is not None else []
                ue = s - EXP_LAG
                if bx is not None and s >= TURN_LAG and (s - TURN_LAG) % 4 == 0:
                    copy_o((s - TURN_LAG) // 4, bx)
                if b2_ is not None and s == 0:
                    copy_o(GR - 1, b2_)
                for i in range(4):
                    if bx is not None and 0 <= ue < UNITS:
                        exp_scores(ue, i, bx)
                    if i == 1:
                        for name in ones[:1]:
                            stage1(name, b1_)
                        if b2_ is not None:
                            for name in STAGE2_AT.get(s - 1, []):
                                tanh_h(name, b2_)
                    if i == 2:
                        for name in ones[1:]:
                            stage1(name, b1_)
                for kind, k in ones:
                    if kind == "q":
                        exp_q(k, b1_)
                for name in twos:
                    stage2(name, b2_)

            run(act, slot)

        @block.vector
        def _(dve):
            for ring in (ring1, ring2, ring_max, ring_exp):
                for free in ring.free:
                    dve.sem_inc(free, 1)
            dve.sem_inc(stored, 16)
            nc.vector.memset(ps_av[:], 0.0)
            nc.vector.memset(ctxT[:], 0.0)
            nc.vector.memset(minus_half[:], -0.5)
            nc.vector.memset(vX[:, :, :, :, HD:HD + 1], 1.0).then_inc(init_ready, 1)

            dve.wait_ge(v1_loaded, 32)
            nc.vector.tensor_copy(v1_hi[:], v1_raw).then_inc(v1_hi_ready, 1)
            dve.wait_ge(v1_hi_ready, 1)
            nc.vector.tensor_tensor(v1_lo[:], v1_raw, v1_hi[:], ALU.subtract).then_inc(v1_ready, 1)

            def layernorm_stats(z, st, mv, k, s_stat, s_mean, b, per, base):
                for i in range(2):
                    t = 2 * k + i
                    nc.vector.bn_stats(out=st[:, t, :], in_=z[:, t, :]).then_inc(s_stat, 1)
                for i in range(2):
                    t = 2 * k + i
                    dve.wait_ge(s_stat, b.count(per, base + t + 1))
                    dve.sem_inc(dve_alone, 1)
                    nc.vector.bn_aggr(out=mv[:, t, :], in_=st[:, t, :]).then_inc(s_mean, 1)

            def normalise(z, mv, rs, s_done):
                for t in range(T):
                    nc.vector.tensor_scalar(z[:, t, :], z[:, t, :], mv[:, t, 0:1], rs[:, t:t + 1], ALU.subtract, ALU.mult)\
                        .then_inc(s_done, 1)

            def stage1(name, b):
                kind, k = name
                ps = ring1.bank(name)
                if name in Q_SUM_AT:
                    sum_q(Q_SUM_AT[name], b)
                if kind == "k":
                    dve.wait_ge(ring1.sem_full(name), ring1.fills(name, b))
                    nc.vector.tensor_reduce(kneg[:, k:k + 1], ps[:], axis=AX.X, op=ALU.max, negate=True).then_inc(kneg_ready, 1)
                if kind == "q":
                    dve.wait_ge(ring1.sem_full(name), ring1.fills(name, b))
                    q3 = ps[:].rearrange("p (h d) -> p h d", d=DH)
                    nc.vector.tensor_reduce(qmax[:, k % 2, :], q3, axis=AX.X, op=ALU.max).then_inc(qmax_ready, 1)
                    dve.wait_ge(qmax_ready, b.count(T, k + 1))
                    if k >= 2:
                        dve.wait_ge(ring1.sem_full(("qT", k - 2)), ring1.fills(("qT", k - 2), b))
                    nc.vector.tensor_tensor(qw[:, k % 2, :].rearrange("p (h d) -> p h d", d=DH), q3,
                                            qmax[:, k % 2, :].unsqueeze(2).broadcast_to([P, HID // DH, DH]), ALU.subtract)\
                        .then_inc(ring1.sem_free(name), 1)
                if kind == "G":
                    dve.wait_ge(ring1.sem_full(name), ring1.fills(name, b))
                    if k == 0:
                        nc.vector.reciprocal(krec[:], ksum[:]).then_inc(krec_ready, 1)
                        dve.wait_ge(krec_ready, b.count(1, 1))
                    for i in range(2):
                        j = 2 * k + i
                        last = nc.vector.tensor_scalar(G[:, j, :], ps[:, i * D:(i + 1) * D], krec[:, j:j + 1], DH ** -0.5,
                                                       ALU.mult, ALU.mult)
                    last.then_inc(ring1.sem_free(name), 1)
                if kind == "o":
                    dve.wait_ge(ring1.sem_full(name), ring1.fills(name, b))
                    dve.wait_ge(resid_ready, b.count(1, 1))
                    z = x1[:, 2 * k:2 * k + 2, :]
                    nc.vector.tensor_tensor(z, ps[:].rearrange("p (t d) -> p t d", d=D), z, ALU.add)\
                        .then_inc(ring1.sem_free(name), 1)
                    dve.wait_ge(ring1.sem_free(name), ring1.reads(name, b))
                    layernorm_stats(x1, st1, mv1, k, stat1, mean1, b, T, 0)
                if kind in ("kX", "qX"):
                    n = k + (2 if kind == "qX" else 0)
                    dve.wait_ge(hi_ready, b.count(4, n + 1))
                    if n >= 2 or not b.first:
                        dve.wait_ge(lo_ready, b.count(4, n - 1))
                    nc.vector.scalar_tensor_tensor(rest[:, k, :], ps[:], HD ** -0.5 if kind == "qX" else 1.0, part[:, k, 0, :],
                                                   ALU.mult, ALU.subtract).then_inc(ring1.sem_free(name), 1)

            def sum_q(t, b):
                dve.wait_ge(qexp_ready, b.count(T, t + 1))
                if t >= 2 or not b.first:
                    dve.wait_ge(qn_ready, b.count(T, t - 1))
                nc.vector.tensor_reduce(qsum[:, t % 2, :], qw[:, t % 2, :].rearrange("p (h d) -> p h d", d=DH), axis=AX.X,
                                        op=ALU.add).then_inc(qsum_ready, 1)
                dve.wait_ge(qsum_ready, b.count(T, t + 1))
                nc.vector.reciprocal(qrec[:, t % 2, :], qsum[:, t % 2, :]).then_inc(qrec_ready, 1)

            def stage2(name, b):
                kind, k = name
                ps = ring2.bank(name)
                if kind in ("y", "f4"):
                    dve.wait_ge(ring2.sem_full(name), ring2.fills(name, b))
                    z = x2[:, 2 * k:2 * k + 2, :]
                    if kind == "y":
                        dve.wait_ge(stored, b.count(16, 16))
                        other = x1b[:, b.parity, 2 * k:2 * k + 2, :]
                        dve.wait_ge(x1b_ready, b.count(1, 1))
                    else:
                        other = z
                        dve.wait_ge(resid2_ready, b.count(1, 1))
                    nc.vector.tensor_tensor(z, ps[:].rearrange("p (t d) -> p t d", d=D), other, ALU.add)\
                        .then_inc(ring2.sem_free(name), 1)
                    dve.wait_ge(ring2.sem_free(name), ring2.reads(name, b))
                    base = 0 if kind == "y" else T
                    layernorm_stats(x2, st2, mv2, k, stat2, mean2, b, 2 * T, base)
                if kind == "f1":
                    dve.wait_ge(p_ready, b.count(1, 1))
                    nc.vector.tensor_tensor(pT[R:2 * R, :], ps[R:2 * R, :], pT[R:2 * R, :], ALU.subtract)\
                        .then_inc(ring2.sem_free(name), 1)
                if name == ("f3", 1):
                    dve.wait_ge(ring2.sem_full(name), ring2.fills(name, b))
                    dve.wait_ge(ring2.sem_free(("f3", 0)), ring2.reads(("f3", 0), b))
                    nc.vector.scalar_tensor_tensor(r2[:], ps[:], 0.5, r2[:], ALU.mult, ALU.add).then_inc(ring2.sem_free(name), 1)

            def gelu_argument(name, b):
                kind, k = name
                if kind == "f2":
                    dve.wait_ge(ring2.sem_free(name), ring2.reads(name, b))
                    dve.wait_ge(hu_ready, b.count(NF, k + 1))
                    nc.vector.scalar_tensor_tensor(hv[:, k % 2, :], hv[:, k % 2, :], 1.0 / GELU_CUBIC, hu[:, k % 2, :],
                                                   ALU.add, ALU.mult).then_inc(hv_ready, 1)

            def gelu_product(name, b):
                kind, k = name
                if kind == "f2":
                    dve.wait_ge(tanh_ready, b.count(NF, k + 1))
                    if k >= 4:
                        dve.wait_ge(ring2.sem_full(("f3", 0)), ring2.fills(("f3", 0), b))
                    nc.vector.scalar_tensor_tensor(h[:, k % 4, :], hv[:, k % 2, :], 1.0, hu[:, k % 2, :], ALU.add, ALU.mult)\
                        .then_inc(h_ready, 1)

            def max_scores(s, i, b):
                g, t = unit_group(s)
                name = ("s", s, i)
                dve.wait_ge(ring_max.sem_full(name), ring_max.fills(name, b))
                nc.vector.tensor_reduce(mx[:, g, i, t:t + 1], ring_max.bank(name)[:], axis=AX.X, op=ALU.max)\
                    .then_inc(ring_max.sem_free(name), 1)

            def split_max(g, b):
                name = ("m", g)
                ps = ring_max.bank(name)[0:4 * T, 0:P]
                dve.wait_ge(ring_max.sem_full(name), ring_max.fills(name, b))
                if g >= 2:
                    dve.wait_ge(maxrow_loaded[g - 2], b.count(48, 48))
                else:
                    if not b.first:
                        dve.wait_ge(maxrow_loaded[g + 2], b.count(48, 0))
                nc.vector.tensor_scalar(mpart[:, g % 2, 0, :], ps, -1.0, None, ALU.mult).then_inc(mhi_ready, 1)
                dve.wait_ge(mhi_ready, b.count(GR, g + 1))
                nc.vector.scalar_tensor_tensor(mrest[:, g % 2, :], ps, -1.0, mpart[:, g % 2, 0, :], ALU.mult, ALU.subtract)\
                    .then_inc(ring_max.sem_free(name), 1)

            def divide_o(g, b):
                dve.wait_ge(o_turned, b.count(GR, g + 1))
                ps = ps_av[:].rearrange("p (t i d) -> p t i d", t=T, i=4)
                nc.vector.reciprocal(orec[:].unsqueeze(3), ps[:, :, :, HD:HD + 1]).then_inc(orec_ready, 1)
                dve.wait_ge(orec_ready, b.count(GR, g + 1))
                if g == 0:
                    for c in range(C):
                        if not b.first:
                            dve.wait_ge(ring2.sem_full(("oT", c)), ring2.fills(("oT", c), b.shifted(-1)))
                nc.vector.tensor_tensor(oN[:, :, 64 * g:64 * (g + 1)].rearrange("p t (i d) -> p t i d", i=4),
                                        ps[:, :, :, 0:HD], orec[:].unsqueeze(3).broadcast_to([P, T, 4, HD]), ALU.mult)\
                    .then_inc(o_ready, 1)

            def slot(s, bx, b1_, b2_):
                ones = STAGE1_AT.get(s, []) if b1_ is not None else []
                twos = STAGE2_AT.get(s, []) if b2_ is not None else []
                twos_before = STAGE2_AT.get(s - 1, []) if b2_ is not None else []
                um = s - MAX_LAG
                for i in range(4):
                    if bx is not None and 0 <= um < UNITS:
                        max_scores(um, i, bx)
                    if i == 0 and bx is not None and um % 4 == 0 and 4 <= um <= UNITS:
                        split_max(um // 4 - 1, bx)
                    if i == 0:
                        for name in twos_before:
                            gelu_argument(name, b2_)
                        if b1_ is not None and s == NORM1_AT:
                            dve.wait_ge(rs1_ready, b1_.count(1, 1))
                            normalise(x1, mv1, rs1, x1_ready)
                        if b2_ is not None and s in (NORM2_AT, NORM3_AT):
                            dve.wait_ge(rs2_ready, b2_.count(2, 1 if s == NORM2_AT else 2))
                            normalise(x2, mv2, rs2, x2_ready)
                    if i == 1:
                        for name in ones[:1]:
                            stage1(name, b1_)
                    if i == 2:
                        if bx is not None and s >= TURN_LAG and (s - TURN_LAG) % 4 == 0:
                            divide_o((s - TURN_LAG) // 4, bx)
                        if b2_ is not None and s == 0:
                            divide_o(GR - 1, b2_)
                        for name in ones[1:]:
                            stage1(name, b1_)
                for name in twos:
                    stage2(name, b2_)
                for name in twos_before:
                    gelu_product(name, b2_)

            run(dve, slot)

        @block.gpsimd
        def _(pool):
            nc.gpsimd.memset(ident[:], 0.0).then_inc(const_ready, 1)
            pool.wait_ge(const_ready, 1)
            nc.gpsimd.affine_select(out=ident[:], in_=ident[:], compare_op=ALU.not_equal, fill=1.0, base=0,
                                    pattern=[[-1, P]], channel_multiplier=1).then_inc(diag_ready, 1)
            pool.wait_ge(diag_ready, 1)
            nc.gpsimd.memset(KS[PROD:PROD + 3, :, :], 1.0).then_inc(ones_ready, 1)
            for dst, src in ((bo_a, a_bo), (bo_c, c_bo), (b2_s, b2)):
                pool.dma_start(dst[:], src.rearrange("(a d) -> a d", a=1).broadcast_to([P, D])).then_inc(rows_loaded, 16)
            pool.wait_ge(ones_ready, 1)
            pool.wait_ge(rows_loaded, 3 * 16)
            pool.wait_ge(init_ready, 1)

            def add_row(dst, src, row, s_done):
                return nc.gpsimd.tensor_tensor(dst, src, row[:].unsqueeze(1).broadcast_to([P, T, D]), ALU.add).then_inc(s_done, 1)

            def rsqrt(mv, sd, rs, s_mean, s_sd, s_done, b, per, more):
                pool.wait_ge(s_mean, b.count(per * T, more * T))
                pool.sem_inc(pool_alone, 1)
                nc.gpsimd.tensor_scalar(sd[:], mv[:, :, 1], EPS, None, ALU.add).then_inc(s_sd, 1)
                pool.wait_ge(s_sd, b.count(per, more))
                pool.sem_inc(pool_alone, 1)
                nc.gpsimd.tensor_tensor(rs[:], sd[:], minus_half[:], ALU.pow).then_inc(s_done, 1)

            def stage1(name, b):
                kind, k = name
                if name == ("xT", 0):
                    pool.wait_ge(x_loaded, b.count(16, 16))
                    pool.sem_inc(pool_alone, 1)
                    if not b.first:
                        pool.wait_ge(x1b_ready, b.count(1, 0))
                        pool.sem_inc(pool_alone, 1)
                    for c in range(C):
                        if not b.first:
                            pool.wait_ge(ring1.sem_full(("x1T", c)), ring1.fills(("x1T", c), b.shifted(-1)))
                            pool.sem_inc(pool_alone, 1)
                    add_row(x1[:], x_s[:], bo_a, resid_ready)
                if kind in ("kX", "qX"):
                    n = k + (2 if kind == "qX" else 0)
                    pool.wait_ge(ring1.sem_free(name), ring1.reads(name, b))
                    pool.sem_inc(pool_alone, 1)
                    nc.gpsimd.tensor_scalar(part[:, k, 1, :], rest[:, k, :], 1.0, None, ALU.mult).then_inc(mid_ready, 1)
                    pool.wait_ge(mid_ready, b.count(4, n + 1))
                    pool.sem_inc(pool_alone, 1)
                    nc.gpsimd.tensor_tensor(part[:, k, 2, :], rest[:, k, :], part[:, k, 1, :], ALU.subtract).then_inc(lo_ready, 1)
                if name == ("o", 1):
                    rsqrt(mv1, sd1, rs1, mean1, sd1_ready, rs1_ready, b, 1, 1)
                if name == ("x1T", 0):
                    pool.wait_ge(x1_ready, b.count(T, T))
                    pool.sem_inc(pool_alone, 1)
                    if b.off >= 2:
                        pool.wait_ge(ring2.sem_free(("y", 1)), ring2.reads(("y", 1), b.shifted(-2)))
                        pool.sem_inc(pool_alone, 1)
                    add_row(x1b[:, b.parity, :, :], x1[:], bo_c, x1b_ready)

            def scale_q(t, b):
                pool.wait_ge(qrec_ready, b.count(T, t + 1))
                pool.sem_inc(pool_alone, 1)
                w = qw[:, t % 2, :].rearrange("p (h d) -> p h d", d=DH)
                nc.gpsimd.tensor_tensor(w, w, qrec[:, t % 2, :].unsqueeze(2).broadcast_to([P, HID // DH, DH]), ALU.mult)\
                    .then_inc(qn_ready, 1)

            def split_max(g, b):
                pool.wait_ge(ring_max.sem_free(("m", g)), ring_max.reads(("m", g), b))
                pool.sem_inc(pool_alone, 1)
                nc.gpsimd.tensor_scalar(mpart[:, g % 2, 1, :], mrest[:, g % 2, :], 1.0, None, ALU.mult).then_inc(mmid_ready, 1)
                pool.wait_ge(mmid_ready, b.count(GR, g + 1))
                pool.sem_inc(pool_alone, 1)
                nc.gpsimd.tensor_tensor(mpart[:, g % 2, 2, :], mrest[:, g % 2, :], mpart[:, g % 2, 1, :], ALU.subtract)\
                    .then_inc(mlo_ready, 1)

            def stage2(name, b):
                if name == ("y", 1):
                    rsqrt(mv2, sd2, rs2, mean2, sd2_ready, rs2_ready, b, 2, 1)
                if name == ("f4", 1):
                    rsqrt(mv2, sd2, rs2, mean2, sd2_ready, rs2_ready, b, 2, 2)
                if name == ("x2T", 1):
                    for c in range(C):
                        pool.wait_ge(ring2.sem_full(("x2T", c)), ring2.fills(("x2T", c), b))
                        pool.sem_inc(pool_alone, 1)
                    pool.wait_ge(x2_ready, b.count(2 * T, T))
                    pool.sem_inc(pool_alone, 1)
                    add_row(x2[:], x2[:], b2_s, resid2_ready)

            def slot(s, bx, b1_, b2_):
                ones = STAGE1_AT.get(s, []) if b1_ is not None else []
                um = s - MAX_LAG
                if bx is not None and um % 4 == 0 and 4 <= um <= UNITS:
                    split_max(um // 4 - 1, bx)
                for name in ones:
                    stage1(name, b1_)
                    if name in Q_SUM_AT:
                        scale_q(Q_SUM_AT[name], b1_)
                for name in STAGE2_AT.get(s, []) if b2_ is not None else []:
                    stage2(name, b2_)

            run(pool, slot)


_INS = ["x", "ctx_768", "L0_attn_Wq", "L0_attn_Wk", "L0_attn_Wv", "L0_attn_Wo", "L0_attn_bo", "L0_xattn_Wq", "L0_xattn_Wk",
        "L0_xattn_Wv", "L0_xattn_Wo", "L0_xattn_bo", "L0_ffn_U1", "L0_ffn_V1", "L0_ffn_b1", "L0_ffn_U2", "L0_ffn_V2", "L0_ffn_b2"]


def kernel(**inputs):
    import numpy as np
    import concourse.bacc as bacc
    from concourse.bass_utils import run_bass_kernel_spmd

    nc = bacc.Bacc("TRN2", target_bir_lowering=False, num_devices=1)
    arrays, args = {}, []
    for name in _INS:
        a = np.ascontiguousarray(inputs[name])
        arrays[f"in_{name}"] = a
        args.append(nc.dram_tensor(f"in_{name}", a.shape, mybir.dt.from_np(a.dtype), kind="ExternalInput").ap())
    out = nc.dram_tensor("out_0", inputs["x"].shape, F32, kind="ExternalOutput").ap()
    decoder_layer(nc, *args, out)
    r = run_bass_kernel_spmd(nc, [arrays], core_ids=[0])
    return r.results[0]["out_0"]
```

```python
from contextlib import ExitStack

import concourse.bass as bass
from concourse import mybir

F32 = mybir.dt.float32
F32R = mybir.dt.float32r
BF16 = mybir.dt.bfloat16
ALU = mybir.AluOpType
ACT = mybir.ActivationFunctionType
AX = mybir.AxisListType

P = 128
EPS = 1e-5
GELU_CUBIC = 0.044715
GELU_SCALE = 0.7978845608028654

STAGE1_AT = {
    1: [("xT", 0), ("xT", 1)], 2: [("q", 0), ("k", 0)], 3: [("k", 1), ("k", 2)], 4: [("q", 1), ("qT", 0)],
    5: [("k", 3), ("q", 2)], 6: [("ek", 0), ("qT", 1)], 7: [("ek", 1), ("q", 3)], 8: [("ek", 2), ("qT", 2)],
    9: [("ek", 3)], 10: [("xTk", 0), ("xTk", 1), ("qT", 3)], 11: [("ctx", 0)], 12: [("G", 0), ("G", 1)],
    13: [("o", 0), ("o", 1)], 15: [("x1T", 0), ("x1T", 1)], 16: [("qX", 0)], 17: [("qX", 1)],
    18: [("cT", 0), ("cT", 1)], 19: [("kX", 0), ("vX", 0)], 20: [("kX", 1), ("vX", 1)],
}
Q_SUM_AT = {("k", 2): 0, ("k", 3): 1, ("ek", 0): 2, ("qT", 2): 3}
STAGE2_AT = {
    1: [("oT", 0), ("oT", 1)], 2: [("y", 0)], 3: [("y", 1)], 5: [("x2T", 0)], 6: [("x2T", 1)], 7: [("f1", 0)],
    8: [("f2", 0)], 9: [("f2", 1)], 10: [("f2", 2)], 11: [("f2", 3)], 12: [("f2", 4)], 13: [("f3", 0), ("f2", 5)],
    14: [("f2", 6)], 15: [("f2", 7)], 17: [("f3", 1)], 18: [("f4", 0)], 19: [("f4", 1)],
}
NORM1_AT, NORM2_AT, NORM3_AT = 14, 5, 20
FIRST_AT = {
    0: [("xT", 0), ("xT", 1)], 1: [("k", 0), ("q", 0)], 2: [("k", 1), ("q", 1)], 3: [("k", 2), ("qT", 0)],
    4: [("k", 3), ("q", 2)], 5: [("ek", 0), ("qT", 1)], 6: [("ek", 1), ("q", 3), ("ek", 2)],
    7: [("qT", 2), ("ek", 3)], 8: [("xTk", 0), ("xTk", 1)], 9: [("qT", 3), ("ctx", 0)],
    10: [("G", 0), ("G", 1), ("o", 0)], 11: [("o", 1), ("cT", 0), ("cT", 1)], 12: [("kX", 0)], 13: [("kX", 1)],
    14: [("x1T", 0), ("x1T", 1)], 17: [("qX", 0), ("qX", 1)], 18: [("vX", 0)], 19: [("vX", 1)],
}
FIRST_SUM_AT = {("k", 1): 0, ("k", 2): 1, ("ek", 0): 2, ("qT", 2): 3}
FIRST_NORM1_AT = 12
SLOTS = 22
MAX_LAG = 0
EXP_LAG = 6
TURN_LAG = EXP_LAG + 5
TURN_AFTER = 2
PE_FIRST, PE_OTHERS, PE_STAGE2 = 0, 1, 2
ACT_FIRST, ACT_OTHERS, ACT_TANH, ACT_STAGE2 = 1, 1, 2, 2
DVE_FIRST, DVE_OTHERS, DVE_ARGUMENT, DVE_PRODUCT, DVE_STAGE2 = 1, 2, 0, 4, 4


class Batch:

    def __init__(self, off, loop=None):
        self.off, self.loop = off, loop

    def shifted(self, by):
        return Batch(self.off + by, self.loop)

    @property
    def parity(self):
        return self.off % 2

    @property
    def first(self):
        return self.loop is None and self.off == 0

    def index(self):
        return self.off if self.loop is None else self.loop * 2 + self.off

    def count(self, per_batch, more):
        if self.loop is None:
            return self.off * per_batch + more
        return self.loop * (2 * per_batch) + (self.off * per_batch + more)


class Ring:

    def __init__(self, order, banks, full, free, start=0):
        self.start = start
        self.place = {name: (n % len(banks), n // len(banks)) for n, name in enumerate(order)}
        self.uses = [len(order[i::len(banks)]) for i in range(len(banks))]
        self.banks, self.full, self.free = banks, full, free

    def bank(self, name):
        return self.banks[self.place[name][0]]

    def sem_full(self, name):
        return self.full[self.place[name][0]]

    def sem_free(self, name):
        return self.free[self.place[name][0]]

    def fills(self, name, batch):
        i, k = self.place[name]
        return batch.shifted(-self.start).count(self.uses[i], k + 1)

    def frees(self, name, batch):
        i, k = self.place[name]
        return batch.shifted(-self.start).count(self.uses[i], k + 1)

    def reads(self, name, batch):
        i, k = self.place[name]
        return batch.shifted(-self.start).count(self.uses[i], k + 2)

    def all_read(self, names, batch, then=None):
        need = {}
        for name in names:
            i, k = self.place[name]
            need[i] = max(need.get(i, 0), k + 2)
        if then is not None:
            i, k = self.place[then]
            need[i] = max(need.get(i, 0), k + 1)
        return [(self.free[i], batch.shifted(-self.start).count(self.uses[i], k)) for i, k in need.items()]


def decoder_layer(nc, x, ctx_768, a_wq, a_wk, a_wv, a_wo, a_bo, c_wq, c_wk, c_wv, c_wo, c_bo,
                  u1, v1, b1, u2, v2, b2, out):
    B, N, D = x.shape
    M, CD = ctx_768.shape[1:]
    HID = a_wq.shape[1]
    DH = 64
    HEADS, HD = 16, D // 16
    R, F = v1.shape
    T = N // P
    C = D // P
    J = HID // P
    GR = HEADS // 4
    NF = F // P
    UNITS = GR * T
    PARTS = 3 * HD
    PROD = 6 * HD
    assert (N, M, D, HID, R, T, C, J) == (512, 512, 256, 512, 64, 4, 2, 4) and B % 2 == 0 and CD == 192

    x_v = x.rearrange("b (p t) d -> b p t d", t=T)
    c_v = ctx_768.rearrange("b (p t) d -> b p t d", t=T)
    out_v = out.rearrange("b (p t) d -> b p t d", t=T)
    q_parts = nc.dram_tensor("q_parts", [HEADS, PARTS, N], BF16, kind="Internal").ap()
    k_parts = nc.dram_tensor("k_parts", [HEADS, PARTS, M], BF16, kind="Internal").ap()

    es = ExitStack()
    with es:
        def sb(name, shape, dt=F32):
            return es.enter_context(nc.sbuf_tensor(name, shape, dt))

        def sem(name):
            return es.enter_context(nc.semaphore(name))

        def sems(name, n):
            return [sem(f"{name}{i}") for i in range(n)]

        wv_a = sb("wv_a", [P, C, HID])
        wk_a, wq_a = sb("wk_a", [P, 2, C, HID], F32R), sb("wq_a", [P, 2, C, HID], F32R)
        wq_c = sb("wq_c", [P, 2, C, D], F32R)
        wo_a = sb("wo_a", [P, J, D])
        wk_c, wv_c, wo_c = (sb(n, [P, C, D]) for n in ("wk_c", "wv_c", "wo_c"))
        u1_s = sb("u1_s", [P, C, 2, R])
        v1_hi, v1_lo = sb("v1_hi", [2 * R, F], F32R), sb("v1_lo", [2 * R, F], F32R)
        u2_s, v2_s = sb("u2_s", [P, NF, R]), sb("v2_s", [2 * R, D])
        b1_s = sb("b1_s", [P, NF])
        bo_a, bo_c, b2_s = sb("bo_a", [P, D]), sb("bo_c", [P, D]), sb("b2_s", [P, D])
        ident = sb("ident", [P, P])
        minus_half = sb("minus_half", [P, T])

        x_s = sb("x_s", [P, T, D])
        c_s = sb("c_s", [P, T, CD])
        tokT = sb("tokT", [P, 2, C, N], F32R)
        ekT = sb("ekT", [P, J, N])
        ek = sb("ek", [P, T, HID])
        kneg, ksum, krec = sb("kneg", [P, J]), sb("ksum", [P, J]), sb("krec", [P, J])
        xTk = sb("xTk", [P, C, HID])
        ctxT = sb("ctxT", [P, J, P])
        G = xTk[:].rearrange("p c (i d) -> p (c i) d", d=D)
        qw = sb("qw", [P, 2, HID])
        qmax, qsum, qrec = (sb(n, [P, 2, HID // DH]) for n in ("qmax", "qsum", "qrec"))
        qT = sb("qT", [P, J, N])
        x1 = sb("x1", [P, T, D])
        st1, mv1, sd1, rs1 = sb("st1", [P, T, 6]), sb("mv1", [P, T, 2]), sb("sd1", [P, T]), sb("rs1", [P, T])
        part = ekT[:].rearrange("p j n -> p (j n)")[:, 0:3 * N].bitcast(BF16).rearrange("p (c i n) -> p c i n", c=2, i=3)
        rest = ek[:, 0:2, :]
        x1b = sb("x1b", [P, 2, T, D])
        vX = sb("vX", [P, 2, T, HEADS, HD + 1])
        QS = sb("QS", [P, HEADS, N], BF16)
        KS = sb("KS", [P, HEADS, M], BF16)
        mx = sb("mx", [P, GR, 4, T])
        mpart = sb("mpart", [4 * T, 2, 3, P], BF16)
        mrest = sb("mrest", [4 * T, 2, P])
        probs = sb("probs", [P, 8, N])
        oTs = sb("oTs", [P, N])
        orec = sb("orec", [P, T, 4])
        oN = sb("oN", [P, T, D])
        oT = sb("oT", [P, C, N])
        x2 = sb("x2", [P, T, D])
        st2, mv2, sd2, rs2 = sb("st2", [P, T, 6]), sb("mv2", [P, T, 2]), sb("sd2", [P, T]), sb("rs2", [P, T])
        pT = sb("pT", [2 * R, N], F32R)
        hu, hv = sb("hu", [P, 2, N]), sb("hv", [P, 2, N])
        h = sb("h", [P, 4, N])
        r2 = sb("r2", [2 * R, N])
        wk_raw, wq_raw = (probs[:, 2 * i:2 * i + 2, :] for i in range(2))
        wqc_raw = probs[:, 4, :].rearrange("p (c n) -> p c n", c=C)
        v1_raw = h[:, 0:2, :].rearrange("p a n -> p (a n)")

        def banks(name, n):
            return [es.enter_context(nc.psum_tensor(f"{name}{i}", [P, 512], F32)) for i in range(n)]

        order1 = [name for s in sorted(STAGE1_AT) for name in STAGE1_AT[s]]
        order1_first = [name for s in sorted(FIRST_AT) for name in FIRST_AT[s]]
        order2 = [name for s in sorted(STAGE2_AT) for name in STAGE2_AT[s]]
        order_max = []
        for u in range(4 * GR + 1):
            for i in range(4):
                order_max += [("s", u, i)] if u < 4 * GR else []
                order_max += [("m", u // 4 - 1)] if u % 4 == 0 and u and i == 0 else []
        order_exp = []
        for u in range(UNITS):
            for i in range(4):
                order_exp.append(("e", u, i))
                order_exp += [("t", (u - 5) // 4)] if u > 4 and u % 4 == 1 and i == TURN_AFTER else []
        order_exp.append(("t", GR - 1))
        ring1 = Ring(order1, banks("ps_one", 2), sems("one_full", 2), sems("one_read", 2), 1)
        ring2 = Ring(order2, banks("ps_two", 1), sems("two_full", 1), sems("two_read", 1))
        ring_max = Ring(order_max, banks("ps_max", 2), sems("max_full", 2), sems("max_read", 2))
        ring_exp = Ring(order_exp, banks("ps_exp", 2), sems("exp_full", 2), sems("exp_read", 2))
        ring_max_last = Ring(order_max, ring_max.banks + ring1.banks, sems("max_last_full", 4), sems("max_last_read", 4), B - 1)
        ring2_last = Ring(order2, ring2.banks + ring_max.banks, sems("two_last_full", 3), sems("two_last_read", 3), B - 1)
        ps_av = banks("ps_av", 1)[0]

        ring1_first = Ring(order1_first, ring1.banks + ring2.banks + ring_exp.banks, sems("first_full", 5), sems("first_read", 5))

        def one_ring(b):
            return ring1_first if b.first else ring1

        def stage1_pieces(s, b):
            return [] if b is None else (FIRST_AT if b.first else STAGE1_AT).get(s, [])

        def slot_of(name, table):
            return next(s for s, names in table.items() if name in names)

        def split_number(name, b):
            order = order1_first if b.first else order1
            return [n for n in order if n[0] in ("kX", "qX")].index(name)

        def splits_before(name, b):
            other = ("qX" if name[0] == "kX" else "kX", name[1])
            if split_number(other, b) < split_number(name, b):
                return b.count(4, split_number(other, b) + 1)
            if b.first:
                return None
            before = b.shifted(-1)
            return before.count(4, 1 + max(split_number(other, before), split_number(name, before)))

        def norm1_at(b):
            return FIRST_NORM1_AT if b.first else NORM1_AT

        def q_sum_at(b):
            return FIRST_SUM_AT if b.first else Q_SUM_AT

        def is_last(b):
            return b.loop is None and b.off == B - 1

        def gelu_buffers(b):
            return (ekT, ek, 4) if is_last(b) else (hu, hv, 2)

        def max_ring(b):
            return ring_max_last if is_last(b) else ring_max

        def two_ring(b):
            return ring2_last if is_last(b) else ring2

        wkc_loaded, wvc_loaded, wka_loaded, wqa_loaded, wva_loaded, woa_loaded, wqc_loaded, woc_loaded, ffn_loaded = (
            sem(n) for n in ("wkc_loaded", "wvc_loaded", "wka_loaded", "wqa_loaded", "wva_loaded", "woa_loaded", "wqc_loaded",
                             "woc_loaded", "ffn_loaded"))
        v1_loaded, v1_ready = sem("v1_loaded"), sem("v1_ready")
        copied_hi_ready = sem("copied_hi_ready")
        whi_ready, wk_ready, wq_ready, wqc_ready = (sem(n) for n in ("whi_ready", "wk_ready", "wq_ready", "wqc_ready"))
        tok_hi_ready = sem("tok_hi_ready")
        p_ready = sem("p_ready")
        ones_ready, const_ready, diag_ready, init_ready = sem("ones_ready"), sem("const_ready"), sem("diag_ready"), sem("init_ready")
        rows_loaded = sem("rows_loaded")
        sp_alone, pool_alone, dve_alone, pe_alone = (sem(n) for n in ("sp_alone", "pool_alone", "dve_alone", "pe_alone"))
        x_loaded, c_loaded, stored = sem("x_loaded"), sem("c_loaded"), sem("stored")
        q_written, k_written = sems("q_written", 2), sems("k_written", 2)
        qstack_loaded, kstack_loaded = sems("qstack_loaded", GR), sems("kstack_loaded", GR)
        maxrow_loaded = sems("maxrow_loaded", GR)
        kneg_ready, krec_ready = sem("kneg_ready"), sem("krec_ready")
        qmax_ready, qexp_ready, qsum_ready, qrec_ready, qn_ready = (sem(n) for n in (
            "qmax_ready", "qexp_ready", "qsum_ready", "qrec_ready", "qn_ready"))
        resid_ready = sem("resid_ready")
        stat1, mean1, sd1_ready, rs1_ready, x1_ready, x1b_ready = (sem(n) for n in (
            "stat1", "mean1", "sd1_ready", "rs1_ready", "x1_ready", "x1b_ready"))
        hi_ready, lo_ready = sem("hi_ready"), sem("lo_ready")
        k_mid_ready, q_mid_ready = sem("k_mid_ready"), sem("q_mid_ready")
        mhi_ready, mmid_ready, mlo_ready = sem("mhi_ready"), sem("mmid_ready"), sem("mlo_ready")
        av_done = sem("av_done")
        o_copied, orec_ready = sem("o_copied"), sem("orec_ready")
        resid2_ready = sem("resid2_ready")
        stat2, mean2, sd2_ready, rs2_ready, x2_ready = (sem(n) for n in (
            "stat2", "mean2", "sd2_ready", "rs2_ready", "x2_ready"))
        hu_ready, hv_ready, tanh_ready, h_ready = sem("hu_ready"), sem("hv_ready"), sem("tanh_ready"), sem("h_ready")

        N_FFN = 6

        def unit_group(u):
            return u // T, u % T

        block = es.enter_context(nc.Block())

        def run(engine, slot, pairs_after=0):
            for s in range(SLOTS):
                slot(s, None, Batch(0), None)
            for s in range(SLOTS):
                slot(s, Batch(0), Batch(1), None)
            pairs = (B - 2) // 2 - pairs_after
            with engine.Fori(0, pairs) as i:
                for off in (1, 2):
                    b = Batch(off, i)
                    for s in range(SLOTS):
                        slot(s, b, b.shifted(1), b.shifted(-1))
            for off in range(2 * pairs + 1, B - 1):
                b = Batch(off)
                for s in range(SLOTS):
                    slot(s, b, b.shifted(1), b.shifted(-1))
            for s in range(SLOTS):
                slot(s, Batch(B - 1), None, Batch(B - 2))
            for s in range(SLOTS):
                slot(s, None, None, Batch(B - 1))

        @block.sync
        def _(sp):
            def weight_in(dst, src, loaded):
                sp.dma_start(dst, src.rearrange("(c p) n -> p c n", p=P)).then_inc(loaded, 16)

            sp.dma_start(x_s[:], x_v[0]).then_inc(x_loaded, 16)
            weight_in(wk_raw, a_wk, wka_loaded)
            weight_in(wq_raw, a_wq, wqa_loaded)
            sp.dma_start(c_s[:], c_v[0]).then_inc(c_loaded, 16)
            for dst, src, loaded in ((wk_c, c_wk, wkc_loaded), (wv_c, c_wv, wvc_loaded)):
                sp.dma_start(dst[:, 0, :], src[0:P, :]).then_inc(loaded, 16)
                sp.dma_start(dst[0:CD - P, 1, :], src[P:CD, :]).then_inc(loaded, 16)
            for dst, src, loaded in ((wv_a[:], a_wv, wva_loaded), (wo_a[:], a_wo, woa_loaded), (wqc_raw, c_wq, wqc_loaded),
                                     (wo_c[:], c_wo, woc_loaded), (u1_s[:, :, 0, :], u1, ffn_loaded),
                                     (u1_s[:, :, 1, :], u1, ffn_loaded)):
                weight_in(dst, src, loaded)
            for half in range(2):
                sp.dma_start(v1_raw[half * R:(half + 1) * R, :], v1).then_inc(v1_loaded, 16)
            sp.dma_start(u2_s[:], u2.rearrange("(p f) r -> p f r", p=P)).then_inc(ffn_loaded, 16)
            for half in range(2):
                sp.dma_start(v2_s[half * R:(half + 1) * R, :], v2).then_inc(ffn_loaded, 16)
            sp.dma_start(b1_s[:], b1.rearrange("(p f) -> p f", p=P)).then_inc(ffn_loaded, 16)

            def context_in(b):
                before = b.shifted(-1)
                for name in (("cT", 1), ("cT", 0)):
                    sp.wait_ge(one_ring(before).sem_full(name), one_ring(before).fills(name, before))
                    sp.sem_inc(sp_alone, 1)
                sp.dma_start(c_s[:], c_v[b.index()]).then_inc(c_loaded, 16)

            def tokens_in(b):
                before = b.shifted(-1)
                for name in (("xTk", 0), ("xTk", 1)):
                    sp.wait_ge(one_ring(before).sem_full(name), one_ring(before).fills(name, before))
                    sp.sem_inc(sp_alone, 1)
                sp.wait_ge(resid_ready, b.count(1, 0))
                sp.sem_inc(sp_alone, 1)
                sp.dma_start(x_s[:], x_v[b.index()]).then_inc(x_loaded, 16)

            def stack_in(dst, src, written, loaded, g, b):
                sp.wait_ge(written[g // 2], b.count(48, 48))
                sp.sem_inc(sp_alone, 1)
                if not b.first:
                    for i in (2, 3):
                        name = ("e", 4 * g + 3, i)
                        sp.wait_ge(ring_exp.sem_full(name), ring_exp.fills(name, b.shifted(-1)))
                        sp.sem_inc(sp_alone, 1)
                hs = slice(4 * g, 4 * g + 4)
                for row, rows in ((0, 3), (3, 2), (5, 1)):
                    at = (3 - rows) * HD if dst is KS else 0
                    sp.dma_start(dst[row * HD:(row + rows) * HD, hs, :],
                                 src[hs, at:at + rows * HD, :].rearrange("h r n -> r h n")).then_inc(loaded[g], 16)

            def q_stack_in(g, b):
                stack_in(QS, q_parts, q_written, qstack_loaded, g, b)

            def k_stack_in(g, b):
                stack_in(KS, k_parts, k_written, kstack_loaded, g, b)

            def parts_out(c, which, b):
                k = split_number((("kX", "qX")[which], c), b)
                dst, written, loaded = ((k_parts, k_written, kstack_loaded), (q_parts, q_written, qstack_loaded))[which]
                for g in (2 * c, 2 * c + 1):
                    if not b.first:
                        sp.wait_ge(loaded[g], b.count(48, 0))
                        sp.sem_inc(sp_alone, 1)
                made = ((hi_ready, b.count(4, k + 1)), (q_mid_ready if which else k_mid_ready, b.count(2, c + 1)),
                        (lo_ready, b.count(4, k + 1)))
                for i, (ready, count) in enumerate(made):
                    sp.wait_ge(ready, count)
                    sp.sem_inc(sp_alone, 1)
                    at = (i if which else 2 - i) * HD
                    sp.dma_start(dst[8 * c:8 * c + 8, at:at + HD, :], part[:, c, i, :]).then_inc(written[c], 16)

            def stack_slot(kind, g, b):
                made = slot_of((kind, g // 2), FIRST_AT if b.first else STAGE1_AT)
                if b.first:
                    last = slot_of(("qX", 1), FIRST_AT)
                    return {"qX": (made, made, SLOTS, SLOTS), "kX": (made, last, last, SLOTS)}[kind][g]
                return max(made, EXP_LAG + 4 * g + 4)

            def slot(s, bx, b1_, b2_):
                g, rest_of = divmod(s - MAX_LAG - 4, 4)
                if bx is not None and rest_of == 0 and 0 <= g < GR:
                    sp.wait_ge(mlo_ready, bx.count(GR, g + 1))
                    sp.sem_inc(sp_alone, 1)
                    for i in range(3):
                        sp.dma_start(QS[PROD + i:PROD + i + 1, 4 * g:4 * g + 4, :].rearrange("a h (t n) -> a (h t) n", n=P),
                                     mpart[:, g % 2, i, :]).then_inc(maxrow_loaded[g], 16)
                if bx is not None and s == 0:
                    for g in range(GR):
                        if stack_slot("qX", g, bx) >= SLOTS:
                            q_stack_in(g, bx)
                    for g in range(GR):
                        if stack_slot("kX", g, bx) >= SLOTS:
                            k_stack_in(g, bx)
                for kind, c in stage1_pieces(s, b1_):
                    if kind in ("kX", "qX"):
                        parts_out(c, 0 if kind == "kX" else 1, b1_)
                    if kind == "qX":
                        for g in (2 * c, 2 * c + 1):
                            if stack_slot("qX", g, b1_) == s:
                                q_stack_in(g, b1_)
                    if kind == "kX":
                        for g in (2 * c, 2 * c + 1):
                            if stack_slot("kX", g, b1_) == s:
                                k_stack_in(g, b1_)
                for g in range(GR):
                    if b1_ is not None and s == stack_slot("qX", g, b1_) and ("qX", g // 2) not in stage1_pieces(s, b1_):
                        q_stack_in(g, b1_)
                    if b1_ is not None and s == stack_slot("kX", g, b1_) and ("kX", g // 2) not in stage1_pieces(s, b1_):
                        k_stack_in(g, b1_)
                if b2_ is not None and s == NORM3_AT:
                    sp.wait_ge(x2_ready, b2_.count(8, 8))
                    sp.sem_inc(sp_alone, 1)
                    sp.dma_start(out_v[b2_.index()], x2[:]).then_inc(stored, 16)
                if b1_ is not None and not is_last(b1_):
                    for name in stage1_pieces(s - 1, b1_):
                        if name == ("cT", 1):
                            context_in(b1_.shifted(1))
                        if name == ("ctx", 0):
                            tokens_in(b1_.shifted(1))

            run(sp, slot, pairs_after=1)
            sp.wait_ge(stored, 16 * (B + 1))

        @block.tensor
        def _(pe):
            pe.wait_ge(diag_ready, 1)
            pe.wait_ge(init_ready, 1)

            def mm(dst, lhsT, rhs, start, stop, **kw):
                return nc.tensor.matmul(dst, lhsT, rhs, start=start, stop=stop, **kw)

            def transpose(dst, src):
                return nc.tensor.transpose(dst, src, ident[0:src.shape[0], 0:src.shape[0]])

            def tile(t):
                return slice(t * P, (t + 1) * P)

            part_products = [(wp, xp, c) for wp, xp in ((1, 0), (0, 1), (0, 0)) for c in range(C)]

            needs1 = {"kX": [("cT", 0), ("cT", 1)], "vX": [("cT", 0), ("cT", 1)], "k": [("xT", 0), ("xT", 1)],
                      "q": [("xT", 0), ("xT", 1)], "ek": [("k", j) for j in range(J)], "xTk": [("ek", t) for t in range(T)],
                      "ctx": [("xTk", c) for c in range(C)], "G": [("ctx", 0)],
                      "o": [("G", 0), ("G", 1)] + [("qT", t) for t in range(T)], "qX": [("x1T", 0), ("x1T", 1)]}
            needs2 = {"y": [("oT", 0), ("oT", 1)], "f1": [("x2T", 0), ("x2T", 1)], "f2": [("f1", 0)], "f4": [("f3", 1)]}

            weights1 = {("kX", 0): wkc_loaded, ("vX", 0): wvc_loaded, ("k", 0): wk_ready, ("q", 0): wq_ready,
                        ("ctx", 0): wva_loaded, ("G", 0): woa_loaded, ("qX", 0): wqc_ready}

            def stage1(name, b):
                kind, k = name
                ps = one_ring(b).bank(name)
                if name == ("cT", 0):
                    pe.wait_ge(c_loaded, b.count(16, 16))
                if b.loop is None and b.off == 1 and name == order1[0]:
                    for read, count in ring1_first.all_read(order1_first, b.shifted(-1)):
                        pe.wait_ge(read, count)
                if name == ("xT", 0):
                    pe.wait_ge(x_loaded, b.count(16, 16))
                if b.first and name in weights1:
                    ready = 32 if kind in ("kX", "vX") else 1 if kind in ("k", "q", "qX") else 16
                    pe.wait_ge(weights1[name], ready)
                if kind == "qT":
                    pe.wait_ge(qn_ready, b.count(T, k + 1))
                if kind == "x1T":
                    pe.wait_ge(x1_ready, b.count(T, T))
                for read, count in one_ring(b).all_read(needs1.get(kind, []), b, then=name):
                    pe.wait_ge(read, count)
                if name == ("cT", 1):
                    pe.sem_inc(pe_alone, 1)
                if kind == "cT":
                    rows = P if k == 0 else CD - P
                    for t in range(T):
                        last = transpose(ps[0:rows, tile(t)], c_s[:, t, k * P:k * P + rows])
                if kind == "kX":
                    for c in range(2):
                        rows = CD - P if c == 1 else P
                        last = mm(ps[:], wk_c[0:rows, c, k * P:(k + 1) * P], oT[0:rows, c, :], c == 0, c == 1)
                if kind == "qX":
                    for n, (wp, xp, c) in enumerate(part_products):
                        last = mm(ps[:], wq_c[:, wp, c, tile(k)], tokT[:, xp, c, :], n == 0, n == 3 * C - 1)
                if kind == "vX":
                    for i in range(2):
                        for c in range(2):
                            rows = CD - P if c == 1 else P
                            last = mm(ps[:, i * D:(i + 1) * D], oT[0:rows, c, tile(2 * k + i)], wv_c[0:rows, c, :],
                                      c == 0, c == 1)
                if kind in ("xT", "x1T"):
                    src = x_s if kind == "xT" else x1
                    for t in range(T):
                        last = transpose(ps[:, tile(t)], src[:, t, k * P:(k + 1) * P])
                if kind == "k":
                    for n, (wp, xp, c) in enumerate(part_products):
                        last = mm(ps[:], wk_a[:, wp, c, tile(k)], tokT[:, xp, c, :], n == 0, n == 3 * C - 1)
                if kind == "q":
                    for n, (wp, xp, c) in enumerate(part_products):
                        last = mm(ps[:], tokT[:, xp, c, tile(k)], wq_a[:, wp, c, :], n == 0, n == 3 * C - 1)
                if kind == "ek":
                    for j in range(J):
                        last = transpose(ps[:, tile(j)], ekT[:, j, tile(k)])
                if kind == "xTk":
                    for t in range(T):
                        last = mm(ps[:], x_s[:, t, k * P:(k + 1) * P], ek[:, t, :], t == 0, t == T - 1)
                if kind == "ctx":
                    for j in range(J):
                        for c in range(C):
                            last = mm(ps[:, tile(j)], wv_a[:, c, tile(j)], xTk[:, c, tile(j)], c == 0, c == C - 1)
                if kind == "G":
                    for i in range(2):
                        last = mm(ps[:, i * D:(i + 1) * D], ctxT[:, 2 * k + i, :], wo_a[:, 2 * k + i, :], True, True)
                if kind == "qT":
                    for j in range(J):
                        last = transpose(ps[:, tile(j)], qw[:, k % 2, tile(j)])
                if kind == "o":
                    for i in range(2):
                        for j in range(J):
                            last = mm(ps[:, i * D:(i + 1) * D], qT[:, j, tile(2 * k + i)], G[:, j, :], j == 0, j == J - 1)
                last.then_inc(one_ring(b).sem_full(name), 1)

            def stage2(name, b):
                kind, k = name
                ps = two_ring(b).bank(name)
                if b.first and name == ("y", 0):
                    pe.wait_ge(woc_loaded, 16)
                if b.first and name == ("f1", 0):
                    pe.wait_ge(ffn_loaded, 16 * N_FFN)
                    pe.wait_ge(v1_ready, 1)
                if kind == "oT":
                    for read, count in ring_exp.all_read([("t", g) for g in range(GR)], b):
                        pe.wait_ge(read, count)
                if is_last(b) and name == ("oT", 0):
                    for read, count in ring2.all_read(order2, b.shifted(-1)) + ring_max_last.all_read(order_max, b):
                        pe.wait_ge(read, count)
                if kind == "x2T":
                    pe.wait_ge(x2_ready, b.count(2 * T, T))
                if kind == "f3":
                    pe.wait_ge(h_ready, b.count(NF, 4 * k + 4))
                for read, count in two_ring(b).all_read(needs2.get(kind, []), b, then=name):
                    pe.wait_ge(read, count)
                if kind in ("oT", "x2T"):
                    src = oN if kind == "oT" else x2
                    for t in range(T):
                        last = transpose(ps[:, tile(t)], src[:, t, k * P:(k + 1) * P])
                if kind == "y":
                    for i in range(2):
                        for c in range(C):
                            last = mm(ps[:, i * D:(i + 1) * D], oT[:, c, tile(2 * k + i)], wo_c[:, c, :], c == 0, c == C - 1)
                if kind == "f1":
                    for c in range(C):
                        last = mm(ps[:], u1_s[:, c, :, :].rearrange("p a r -> p (a r)"), oT[:, c, :], c == 0, c == C - 1)
                if kind == "f2":
                    mm(ps[:], v1_lo[:, k::NF], pT[:], True, False)
                    last = mm(ps[:], v1_hi[:, k::NF], pT[:], False, True)
                if kind == "f3":
                    for i in range(4):
                        half = i % 2
                        last = mm(ps[half * R:(half + 1) * R, :], u2_s[:, 4 * k + i, :], h[:, i, :], i < 2, i >= 2)
                if kind == "f4":
                    for i in range(2):
                        last = mm(ps[:, i * D:(i + 1) * D], r2[:, tile(2 * k + i)], v2_s[:], True, True)
                last.then_inc(two_ring(b).sem_full(name), 1)

            def scores_for_max(s, i, b):
                g, t = unit_group(s)
                name, head = ("s", s, i), 4 * g + i
                if i == 0 and t == 0:
                    pe.wait_ge(qstack_loaded[g], b.count(48, 48))
                    pe.wait_ge(kstack_loaded[g], b.count(48, 48))
                if is_last(b) and s == 0 and i == 0:
                    for read, count in ring1.all_read(order1, b) + ring_max.all_read(order_max, b.shifted(-1)):
                        pe.wait_ge(read, count)
                pe.wait_ge(max_ring(b).sem_free(name), max_ring(b).frees(name, b))
                mm(max_ring(b).bank(name)[:], QS[0:PROD, head, tile(t)], KS[0:PROD, head, :], True, True)\
                    .then_inc(max_ring(b).sem_full(name), 1)

            def turn_max(g, b):
                name = ("m", g)
                for read, count in max_ring(b).all_read([("s", 4 * g + 3, 2), ("s", 4 * g + 3, 3)], b, then=name):
                    pe.wait_ge(read, count)
                transpose(max_ring(b).bank(name)[0:4 * T, 0:P], mx[:, g, :, :].rearrange("p h t -> p (h t)"))\
                    .then_inc(max_ring(b).sem_full(name), 1)

            def scores_for_exp(u, i, b):
                g, mc = unit_group(u)
                name, head = ("e", u, i), 4 * g + i
                if u == 0 and i == 0 and b.first:
                    pe.wait_ge(ones_ready, 1)
                if i == 0 and mc == 0:
                    pe.wait_ge(maxrow_loaded[g], b.count(48, 48))
                pe.wait_ge(ring_exp.sem_free(name), ring_exp.frees(name, b))
                mm(ring_exp.bank(name)[:], KS[0:PROD + 3, head, tile(mc)], QS[0:PROD + 3, head, :], True, True)\
                    .then_inc(ring_exp.sem_full(name), 1)

            def probs_times_v(u, b):
                g, mc = unit_group(u)
                if mc == 0:
                    if g or not b.first:
                        pe.wait_ge(o_copied, b.count(GR, g))
                    if g == 0:
                        for read, count in one_ring(b).all_read([("vX", 0), ("vX", 1)], b):
                            pe.wait_ge(read, count)
                for read, count in ring_exp.all_read([("e", u, i) for i in range(4)], b):
                    pe.wait_ge(read, count)
                for i in range(4):
                    last = mm(ps_av[32 * i:32 * i + HD + 1, :], vX[:, b.parity, mc, 4 * g + i, :],
                              probs[:, 4 * (u % 2) + i, :], mc == 0, mc == T - 1, tile_position=(0, 32 * i))
                last.then_inc(av_done, 1)

            def turn_o(g, b):
                name = ("t", g)
                pe.wait_ge(o_copied, b.count(GR, g + 1))
                pe.wait_ge(ring_exp.sem_free(name), ring_exp.frees(name, b))
                for t in range(T):
                    last = transpose(ring_exp.bank(name)[:, tile(t)], oTs[:, tile(t)])
                last.then_inc(ring_exp.sem_full(name), 1)

            def slot(s, bx, b1_, b2_):
                ones = stage1_pieces(s, b1_)
                twos = STAGE2_AT.get(s, []) if b2_ is not None else []
                um, ue = s - MAX_LAG, s - EXP_LAG
                if b2_ is not None and s == 0:
                    probs_times_v(UNITS - 1, b2_)
                for i in range(4):
                    if bx is not None and 0 <= um < UNITS:
                        scores_for_max(um, i, bx)
                    if i == 0 and bx is not None and um % 4 == 0 and 4 <= um <= UNITS:
                        turn_max(um // 4 - 1, bx)
                    if bx is not None and 0 <= ue < UNITS:
                        scores_for_exp(ue, i, bx)
                    if i == PE_FIRST:
                        for name in ones[:1]:
                            stage1(name, b1_)
                    if i == TURN_AFTER:
                        if bx is not None and s >= TURN_LAG and (s - TURN_LAG) % 4 == 0:
                            turn_o((s - TURN_LAG) // 4, bx)
                        if b2_ is not None and s == 0:
                            turn_o(GR - 1, b2_)
                    if i == PE_OTHERS:
                        for name in ones[1:]:
                            stage1(name, b1_)
                    if i == PE_STAGE2:
                        for name in twos[:1]:
                            stage2(name, b2_)
                for name in twos[1:]:
                    stage2(name, b2_)
                if bx is not None and 1 <= ue <= UNITS - 1:
                    probs_times_v(ue - 1, bx)

            run(pe, slot)

        @block.scalar
        def _(act):
            def stage1(name, b):
                kind, k = name
                ps = one_ring(b).bank(name)
                if kind in ("G", "o", "q"):
                    return
                act.wait_ge(one_ring(b).sem_full(name), one_ring(b).fills(name, b))
                if kind == "cT":
                    rows = CD - P if k == 1 else P
                    nc.scalar.activation(oT[0:rows, k, :], ps[0:rows, :], ACT.Copy).then_inc(one_ring(b).sem_free(name), 1)
                if kind in ("xT", "x1T"):
                    nc.scalar.activation(tokT[:, 0, k, :], ps[:], ACT.Copy).then_inc(tok_hi_ready, 1)
                    if name == ("xT", 1) and b.first:
                        high_part(wq_raw, wq_a, wqa_loaded)
                if kind in ("kX", "qX"):
                    n = split_number(name, b)
                    for other, written in (("kX", k_written), ("qX", q_written)):
                        if other != kind and split_number((other, k), b) < n:
                            act.wait_ge(written[k], b.count(48, 48))
                        else:
                            if not b.first:
                                act.wait_ge(written[k], b.count(48, 0))
                    nc.scalar.activation(part[:, k, 0, :], ps[:], ACT.Copy, scale=HD ** -0.5 if kind == "qX" else 1.0)\
                        .then_inc(hi_ready, 1)
                if kind == "vX":
                    nc.scalar.activation(vX[:, b.parity, 2 * k:2 * k + 2, :, 0:HD],
                                         ps[:].rearrange("p (t h d) -> p t h d", t=2, h=HEADS), ACT.Copy)\
                        .then_inc(one_ring(b).sem_free(name), 1)
                if name == ("k", 0) and not b.first:
                    for written in q_written + k_written:
                        act.wait_ge(written, b.count(48, 0))
                if name == ("ek", 0):
                    if not b.first:
                        act.wait_ge(lo_ready, b.count(4, 0))
                if kind == "k":
                    act.wait_ge(kneg_ready, b.count(J, k + 1))
                    nc.scalar.activation(ekT[:, k, :], ps[:], ACT.Exp, bias=kneg[:, k:k + 1], accum_out=ksum[:, k:k + 1])\
                        .then_inc(one_ring(b).sem_free(name), 1)
                if kind in ("ek", "xTk"):
                    dst = ek if kind == "ek" else xTk
                    nc.scalar.activation(dst[:, k, :], ps[:], ACT.Copy).then_inc(one_ring(b).sem_free(name), 1)
                if kind == "ctx":
                    for i in range(2):
                        at = slice(i * DH, (i + 1) * DH)
                        last = nc.scalar.activation(ctxT[at, :, at], ps[at, :].rearrange("p (j d) -> p j d", d=P)[:, :, at],
                                                    ACT.Copy)
                    last.then_inc(one_ring(b).sem_free(name), 1)
                if kind == "qT":
                    nc.scalar.activation(qT[:, :, k * P:(k + 1) * P], ps[:].rearrange("p (j n) -> p j n", n=P), ACT.Copy)\
                        .then_inc(one_ring(b).sem_free(name), 1)

            def middle_of_q(k, b):
                act.wait_ge(one_ring(b).sem_free(("qX", k)), one_ring(b).reads(("qX", k), b))
                nc.scalar.activation(part[:, k, 1, :], rest[:, k, :], ACT.Copy).then_inc(q_mid_ready, 1)

            def exp_q(t, b):
                act.wait_ge(one_ring(b).sem_free(("q", t)), one_ring(b).reads(("q", t), b))
                nc.scalar.activation(qw[:, t % 2, :], qw[:, t % 2, :], ACT.Exp).then_inc(qexp_ready, 1)

            def stage2(name, b):
                kind, k = name
                ps = two_ring(b).bank(name)
                if kind in ("y", "f4") or name == ("f3", 1):
                    return
                act.wait_ge(two_ring(b).sem_full(name), two_ring(b).fills(name, b))
                free = two_ring(b).sem_free(name)
                if kind in ("oT", "x2T"):
                    nc.scalar.activation(oT[:, k, :], ps[:], ACT.Copy).then_inc(free, 1)
                if kind == "f1":
                    nc.scalar.activation(pT[:], ps[:], ACT.Copy).then_inc(p_ready, 1)
                if kind == "f2":
                    arg, th, depth = gelu_buffers(b)
                    if k >= depth:
                        act.wait_ge(h_ready, b.count(NF, k - depth + 1))
                    if b.first and k == 0:
                        act.wait_ge(ffn_loaded, 16 * N_FFN)
                    nc.scalar.activation(arg[:, k % depth, :], ps[:], ACT.Identity, bias=b1_s[:, k:k + 1]).then_inc(hu_ready, 1)
                    nc.scalar.activation(th[:, k % depth, :], ps[:], ACT.Square, bias=b1_s[:, k:k + 1]).then_inc(free, 1)
                if kind == "f3":
                    nc.scalar.activation(r2[:], ps[:], ACT.Copy, scale=0.5).then_inc(free, 1)

            def tanh_h(name, b):
                kind, k = name
                if kind == "f2":
                    _, th, depth = gelu_buffers(b)
                    act.wait_ge(hv_ready, b.count(NF, k + 1))
                    nc.scalar.activation(th[:, k % depth, :], th[:, k % depth, :], ACT.Tanh, scale=GELU_SCALE * GELU_CUBIC)\
                        .then_inc(tanh_ready, 1)

            def exp_scores(u, i, b):
                name = ("e", u, i)
                if b.first and u == 0 and i == 0:
                    act.wait_ge(wk_ready, 1)
                    act.wait_ge(wq_ready, 1)
                    act.wait_ge(wqc_ready, 1)
                if u >= 2 or not b.first:
                    act.wait_ge(av_done, b.count(UNITS, u - 1))
                act.wait_ge(ring_exp.sem_full(name), ring_exp.fills(name, b))
                nc.scalar.activation(probs[:, 4 * (u % 2) + i, :], ring_exp.bank(name)[:], ACT.Exp)\
                    .then_inc(ring_exp.sem_free(name), 1)

            def copy_o(g, b):
                act.wait_ge(av_done, b.count(UNITS, 4 * (g + 1)))
                nc.scalar.activation(oTs[:], ps_av[:], ACT.Copy).then_inc(o_copied, 1)

            act.wait_ge(init_ready, 1)
            def high_part(raw, w, loaded):
                act.wait_ge(loaded, 16)
                nc.scalar.activation(w[:, 0], raw, ACT.Copy).then_inc(whi_ready, 1)

            high_part(wk_raw, wk_a, wka_loaded)

            def slot(s, bx, b1_, b2_):
                ones = stage1_pieces(s, b1_)
                twos = STAGE2_AT.get(s, []) if b2_ is not None else []
                ue = s - EXP_LAG
                if bx is not None and s >= TURN_LAG and (s - TURN_LAG) % 4 == 0:
                    copy_o((s - TURN_LAG) // 4, bx)
                if b2_ is not None and s == 0:
                    copy_o(GR - 1, b2_)
                for i in range(4):
                    if bx is not None and 0 <= ue < UNITS:
                        exp_scores(ue, i, bx)
                    if i == ACT_FIRST:
                        for name in ones[:1]:
                            stage1(name, b1_)
                            if name[0] == "qX" and b1_.first:
                                middle_of_q(name[1], b1_)
                    if i == ACT_TANH:
                        if b2_ is not None and not is_last(b2_):
                            for name in STAGE2_AT.get(s - 1, []):
                                tanh_h(name, b2_)
                    if i == ACT_OTHERS:
                        for name in ones[1:]:
                            stage1(name, b1_)
                            if name[0] == "qX" and b1_.first:
                                middle_of_q(name[1], b1_)
                    if i == ACT_STAGE2:
                        for name in twos:
                            stage2(name, b2_)
                for kind, k in ones:
                    if kind == "q":
                        exp_q(k, b1_)
                    if kind == "qX" and not b1_.first:
                        middle_of_q(k, b1_)
                if ACT_STAGE2 > 3:
                    for name in twos:
                        stage2(name, b2_)
                if b2_ is not None and is_last(b2_):
                    for name in STAGE2_AT.get(s - 1, []):
                        tanh_h(name, b2_)

            run(act, slot)

        @block.vector
        def _(dve):
            for ring in (ring1, ring2, ring_max, ring_exp, ring_max_last, ring2_last, ring1_first):
                for free in ring.free:
                    dve.sem_inc(free, 1)
            dve.sem_inc(stored, 16)
            nc.vector.memset(ps_av[:], 0.0)
            nc.vector.memset(ctxT[:], 0.0)
            nc.vector.memset(minus_half[:], -0.5)
            nc.vector.memset(vX[:, :, :, :, HD:HD + 1], 1.0).then_inc(init_ready, 1)

            def low_part(raw, w, n, ready):
                dve.wait_ge(whi_ready, n + 1)
                nc.vector.tensor_tensor(w[:, 1], raw, w[:, 0], ALU.subtract).then_inc(ready, 1)

            low_part(wk_raw, wk_a, 0, wk_ready)

            def split_wq_c():
                dve.wait_ge(wqc_loaded, 16)
                nc.vector.tensor_copy(wq_c[:, 0], wqc_raw).then_inc(copied_hi_ready, 1)
                dve.wait_ge(copied_hi_ready, 1)
                nc.vector.tensor_tensor(wq_c[:, 1], wqc_raw, wq_c[:, 0], ALU.subtract).then_inc(wqc_ready, 1)

            def split_v1():
                dve.wait_ge(v1_loaded, 32)
                nc.vector.tensor_copy(v1_hi[:], v1_raw).then_inc(copied_hi_ready, 1)
                dve.wait_ge(copied_hi_ready, 2)
                nc.vector.tensor_tensor(v1_lo[:], v1_raw, v1_hi[:], ALU.subtract).then_inc(v1_ready, 1)

            def layernorm_stats(z, st, mv, k, s_stat, s_mean, b, per, base):
                for i in range(2):
                    t = 2 * k + i
                    nc.vector.bn_stats(out=st[:, t, :], in_=z[:, t, :]).then_inc(s_stat, 1)
                for i in range(2):
                    t = 2 * k + i
                    dve.wait_ge(s_stat, b.count(per, base + t + 1))
                    dve.sem_inc(dve_alone, 1)
                    nc.vector.bn_aggr(out=mv[:, t, :], in_=st[:, t, :]).then_inc(s_mean, 1)

            def normalise(z, mv, rs, s_done):
                for t in range(T):
                    nc.vector.tensor_scalar(z[:, t, :], z[:, t, :], mv[:, t, 0:1], rs[:, t:t + 1], ALU.subtract, ALU.mult)\
                        .then_inc(s_done, 1)

            def stage1(name, b):
                kind, k = name
                ps = one_ring(b).bank(name)
                if name == ("G", 1) and b.first:
                    split_wq_c()
                if kind in ("xT", "x1T"):
                    dve.wait_ge(tok_hi_ready, b.count(2 * C, k + 1 + (C if kind == "x1T" else 0)))
                    nc.vector.tensor_tensor(tokT[:, 1, k, :], ps[:], tokT[:, 0, k, :], ALU.subtract)\
                        .then_inc(one_ring(b).sem_free(name), 1)
                    if name == ("xT", 1) and b.first:
                        low_part(wq_raw, wq_a, 1, wq_ready)
                if name in q_sum_at(b):
                    sum_q(q_sum_at(b)[name], b)
                if kind == "k":
                    dve.wait_ge(one_ring(b).sem_full(name), one_ring(b).fills(name, b))
                    nc.vector.tensor_reduce(kneg[:, k:k + 1], ps[:], axis=AX.X, op=ALU.max, negate=True).then_inc(kneg_ready, 1)
                if kind == "q":
                    dve.wait_ge(one_ring(b).sem_full(name), one_ring(b).fills(name, b))
                    q3 = ps[:].rearrange("p (h d) -> p h d", d=DH)
                    nc.vector.tensor_reduce(qmax[:, k % 2, :], q3, axis=AX.X, op=ALU.max).then_inc(qmax_ready, 1)
                    dve.wait_ge(qmax_ready, b.count(T, k + 1))
                    if k >= 2:
                        dve.wait_ge(one_ring(b).sem_full(("qT", k - 2)), one_ring(b).fills(("qT", k - 2), b))
                    nc.vector.tensor_tensor(qw[:, k % 2, :].rearrange("p (h d) -> p h d", d=DH), q3,
                                            qmax[:, k % 2, :].unsqueeze(2).broadcast_to([P, HID // DH, DH]), ALU.subtract)\
                        .then_inc(one_ring(b).sem_free(name), 1)
                if kind == "G":
                    dve.wait_ge(one_ring(b).sem_full(name), one_ring(b).fills(name, b))
                    if k == 0:
                        nc.vector.reciprocal(krec[:], ksum[:]).then_inc(krec_ready, 1)
                        dve.wait_ge(krec_ready, b.count(1, 1))
                    for i in range(2):
                        j = 2 * k + i
                        last = nc.vector.tensor_scalar(G[:, j, :], ps[:, i * D:(i + 1) * D], krec[:, j:j + 1], DH ** -0.5,
                                                       ALU.mult, ALU.mult)
                    last.then_inc(one_ring(b).sem_free(name), 1)
                if kind == "o":
                    dve.wait_ge(one_ring(b).sem_full(name), one_ring(b).fills(name, b))
                    dve.wait_ge(resid_ready, b.count(1, 1))
                    z = x1[:, 2 * k:2 * k + 2, :]
                    nc.vector.tensor_tensor(z, ps[:].rearrange("p (t d) -> p t d", d=D), z, ALU.add)\
                        .then_inc(one_ring(b).sem_free(name), 1)
                    dve.wait_ge(one_ring(b).sem_free(name), one_ring(b).reads(name, b))
                    layernorm_stats(x1, st1, mv1, k, stat1, mean1, b, T, 0)
                if kind in ("kX", "qX"):
                    dve.wait_ge(hi_ready, b.count(4, split_number(name, b) + 1))
                    done = splits_before(name, b)
                    if done is not None:
                        dve.wait_ge(lo_ready, done)
                    nc.vector.scalar_tensor_tensor(rest[:, k, :], ps[:], HD ** -0.5 if kind == "qX" else 1.0, part[:, k, 0, :],
                                                   ALU.mult, ALU.subtract).then_inc(one_ring(b).sem_free(name), 1)

            def sum_q(t, b):
                dve.wait_ge(qexp_ready, b.count(T, t + 1))
                if t >= 2 or not b.first:
                    dve.wait_ge(qn_ready, b.count(T, t - 1))
                nc.vector.tensor_reduce(qsum[:, t % 2, :], qw[:, t % 2, :].rearrange("p (h d) -> p h d", d=DH), axis=AX.X,
                                        op=ALU.add).then_inc(qsum_ready, 1)
                dve.wait_ge(qsum_ready, b.count(T, t + 1))
                nc.vector.reciprocal(qrec[:, t % 2, :], qsum[:, t % 2, :]).then_inc(qrec_ready, 1)

            def stage2(name, b):
                kind, k = name
                ps = two_ring(b).bank(name)
                if kind in ("y", "f4"):
                    dve.wait_ge(two_ring(b).sem_full(name), two_ring(b).fills(name, b))
                    z = x2[:, 2 * k:2 * k + 2, :]
                    if kind == "y":
                        dve.wait_ge(stored, b.count(16, 16))
                        other = x1b[:, b.parity, 2 * k:2 * k + 2, :]
                        dve.wait_ge(x1b_ready, b.count(1, 1))
                    else:
                        other = z
                        dve.wait_ge(resid2_ready, b.count(1, 1))
                    nc.vector.tensor_tensor(z, ps[:].rearrange("p (t d) -> p t d", d=D), other, ALU.add)\
                        .then_inc(two_ring(b).sem_free(name), 1)
                    dve.wait_ge(two_ring(b).sem_free(name), two_ring(b).reads(name, b))
                    base = 0 if kind == "y" else T
                    layernorm_stats(x2, st2, mv2, k, stat2, mean2, b, 2 * T, base)
                if kind == "f1":
                    dve.wait_ge(p_ready, b.count(1, 1))
                    nc.vector.tensor_tensor(pT[R:2 * R, :], ps[R:2 * R, :], pT[R:2 * R, :], ALU.subtract)\
                        .then_inc(two_ring(b).sem_free(name), 1)
                if name == ("f3", 1):
                    dve.wait_ge(two_ring(b).sem_full(name), two_ring(b).fills(name, b))
                    dve.wait_ge(two_ring(b).sem_free(("f3", 0)), two_ring(b).reads(("f3", 0), b))
                    nc.vector.scalar_tensor_tensor(r2[:], ps[:], 0.5, r2[:], ALU.mult, ALU.add).then_inc(two_ring(b).sem_free(name), 1)

            def gelu_argument(name, b):
                kind, k = name
                if kind == "f2":
                    arg, th, depth = gelu_buffers(b)
                    dve.wait_ge(two_ring(b).sem_free(name), two_ring(b).reads(name, b))
                    dve.wait_ge(hu_ready, b.count(NF, k + 1))
                    nc.vector.scalar_tensor_tensor(th[:, k % depth, :], th[:, k % depth, :], 1.0 / GELU_CUBIC, arg[:, k % depth, :],
                                                   ALU.add, ALU.mult).then_inc(hv_ready, 1)

            def gelu_product(name, b):
                kind, k = name
                if kind == "f2":
                    arg, th, depth = gelu_buffers(b)
                    dve.wait_ge(tanh_ready, b.count(NF, k + 1))
                    if k >= 4:
                        dve.wait_ge(two_ring(b).sem_full(("f3", 0)), two_ring(b).fills(("f3", 0), b))
                    nc.vector.scalar_tensor_tensor(h[:, k % 4, :], th[:, k % depth, :], 1.0, arg[:, k % depth, :], ALU.add, ALU.mult)\
                        .then_inc(h_ready, 1)

            def max_scores(s, i, b):
                g, t = unit_group(s)
                name = ("s", s, i)
                dve.wait_ge(max_ring(b).sem_full(name), max_ring(b).fills(name, b))
                nc.vector.tensor_reduce(mx[:, g, i, t:t + 1], max_ring(b).bank(name)[:], axis=AX.X, op=ALU.max)\
                    .then_inc(max_ring(b).sem_free(name), 1)

            def split_max(g, b):
                name = ("m", g)
                ps = max_ring(b).bank(name)[0:4 * T, 0:P]
                dve.wait_ge(max_ring(b).sem_full(name), max_ring(b).fills(name, b))
                if g >= 2:
                    dve.wait_ge(maxrow_loaded[g - 2], b.count(48, 48))
                else:
                    if not b.first:
                        dve.wait_ge(maxrow_loaded[g + 2], b.count(48, 0))
                nc.vector.tensor_scalar(mpart[:, g % 2, 0, :], ps, -1.0, None, ALU.mult).then_inc(mhi_ready, 1)
                dve.wait_ge(mhi_ready, b.count(GR, g + 1))
                nc.vector.scalar_tensor_tensor(mrest[:, g % 2, :], ps, -1.0, mpart[:, g % 2, 0, :], ALU.mult, ALU.subtract)\
                    .then_inc(max_ring(b).sem_free(name), 1)

            def divide_o(g, b):
                name = ("t", g)
                dve.wait_ge(ring_exp.sem_full(name), ring_exp.fills(name, b))
                ps = ring_exp.bank(name)[:].rearrange("p (t i d) -> p t i d", t=T, i=4)
                nc.vector.reciprocal(orec[:].unsqueeze(3), ps[:, :, :, HD:HD + 1]).then_inc(orec_ready, 1)
                dve.wait_ge(orec_ready, b.count(GR, g + 1))
                if g == 0:
                    for c in range(C):
                        if not b.first:
                            before = b.shifted(-1)
                            dve.wait_ge(two_ring(before).sem_full(("oT", c)), two_ring(before).fills(("oT", c), before))
                nc.vector.tensor_tensor(oN[:, :, 64 * g:64 * (g + 1)].rearrange("p t (i d) -> p t i d", i=4),
                                        ps[:, :, :, 0:HD], orec[:].unsqueeze(3).broadcast_to([P, T, 4, HD]), ALU.mult)\
                    .then_inc(ring_exp.sem_free(name), 1)

            def slot(s, bx, b1_, b2_):
                ones = stage1_pieces(s, b1_)
                twos = STAGE2_AT.get(s, []) if b2_ is not None else []
                twos_before = STAGE2_AT.get(s - 1, []) if b2_ is not None else []
                um = s - MAX_LAG
                for i in range(4):
                    if bx is not None and 0 <= um < UNITS:
                        max_scores(um, i, bx)
                    if i == 0 and bx is not None and um % 4 == 0 and 4 <= um <= UNITS:
                        split_max(um // 4 - 1, bx)
                    if i == DVE_ARGUMENT:
                        for name in twos_before:
                            if not is_last(b2_):
                                gelu_argument(name, b2_)
                    if i == 0:
                        if b1_ is not None and s == norm1_at(b1_):
                            dve.wait_ge(rs1_ready, b1_.count(1, 1))
                            normalise(x1, mv1, rs1, x1_ready)
                        if b2_ is not None and s in (NORM2_AT, NORM3_AT):
                            dve.wait_ge(rs2_ready, b2_.count(2, 1 if s == NORM2_AT else 2))
                            normalise(x2, mv2, rs2, x2_ready)
                    if i == DVE_FIRST:
                        for name in ones[:1]:
                            stage1(name, b1_)
                    if i == TURN_AFTER + 1:
                        if bx is not None and s >= TURN_LAG and (s - TURN_LAG) % 4 == 0:
                            divide_o((s - TURN_LAG) // 4, bx)
                        if b2_ is not None and s == 0:
                            divide_o(GR - 1, b2_)
                    if i == DVE_OTHERS:
                        for name in ones[1:]:
                            stage1(name, b1_)
                    last = b2_ is not None and is_last(b2_)
                    if i == DVE_STAGE2 and not last:
                        for name in twos:
                            stage2(name, b2_)
                    if i == DVE_PRODUCT and not last:
                        for name in twos_before:
                            gelu_product(name, b2_)
                if DVE_STAGE2 > 3 or last:
                    for name in twos:
                        stage2(name, b2_)
                        if last:
                            gelu_argument(name, b2_)
                if DVE_PRODUCT > 3 or last:
                    for name in twos_before:
                        gelu_product(name, b2_)
                if bx is None and b1_ is not None and s == norm1_at(b1_):
                    split_v1()

            run(dve, slot)

        @block.gpsimd
        def _(pool):
            nc.gpsimd.memset(ident[:], 0.0).then_inc(const_ready, 1)
            pool.wait_ge(const_ready, 1)
            nc.gpsimd.affine_select(out=ident[:], in_=ident[:], compare_op=ALU.not_equal, fill=1.0, base=0,
                                    pattern=[[-1, P]], channel_multiplier=1).then_inc(diag_ready, 1)
            pool.wait_ge(diag_ready, 1)
            nc.gpsimd.memset(KS[PROD:PROD + 3, :, :], 1.0).then_inc(ones_ready, 1)
            for dst, src in ((bo_a, a_bo), (bo_c, c_bo), (b2_s, b2)):
                pool.dma_start(dst[:], src.rearrange("(a d) -> a d", a=1).broadcast_to([P, D])).then_inc(rows_loaded, 16)
            pool.wait_ge(ones_ready, 1)
            pool.wait_ge(rows_loaded, 3 * 16)
            pool.wait_ge(init_ready, 1)

            def add_row(dst, src, row, s_done):
                return nc.gpsimd.tensor_tensor(dst, src, row[:].unsqueeze(1).broadcast_to([P, T, D]), ALU.add).then_inc(s_done, 1)

            def rsqrt(mv, sd, rs, s_mean, s_sd, s_done, b, per, more):
                pool.wait_ge(s_mean, b.count(per * T, more * T))
                pool.sem_inc(pool_alone, 1)
                nc.gpsimd.tensor_scalar(sd[:], mv[:, :, 1], EPS, None, ALU.add).then_inc(s_sd, 1)
                pool.wait_ge(s_sd, b.count(per, more))
                pool.sem_inc(pool_alone, 1)
                nc.gpsimd.tensor_tensor(rs[:], sd[:], minus_half[:], ALU.pow).then_inc(s_done, 1)

            def stage1(name, b):
                kind, k = name
                if name == ("xT", 0):
                    pool.wait_ge(x_loaded, b.count(16, 16))
                    pool.sem_inc(pool_alone, 1)
                    if not b.first:
                        pool.wait_ge(x1b_ready, b.count(1, 0))
                        pool.sem_inc(pool_alone, 1)
                    for c in range(C):
                        if not b.first:
                            before = b.shifted(-1)
                            pool.wait_ge(one_ring(before).sem_full(("x1T", c)), one_ring(before).fills(("x1T", c), before))
                            pool.sem_inc(pool_alone, 1)
                    add_row(x1[:], x_s[:], bo_a, resid_ready)
                if kind in ("kX", "qX"):
                    if kind == "kX":
                        pool.wait_ge(one_ring(b).sem_free(name), one_ring(b).reads(name, b))
                        pool.sem_inc(pool_alone, 1)
                        nc.gpsimd.tensor_scalar(part[:, k, 1, :], rest[:, k, :], 1.0, None, ALU.mult).then_inc(k_mid_ready, 1)
                    pool.wait_ge(k_mid_ready if kind == "kX" else q_mid_ready, b.count(2, k + 1))
                    pool.sem_inc(pool_alone, 1)
                    nc.gpsimd.tensor_tensor(part[:, k, 2, :], rest[:, k, :], part[:, k, 1, :], ALU.subtract).then_inc(lo_ready, 1)
                if name == ("o", 1):
                    rsqrt(mv1, sd1, rs1, mean1, sd1_ready, rs1_ready, b, 1, 1)
                if name == ("qX", 1):
                    pool.wait_ge(x1_ready, b.count(T, T))
                    pool.sem_inc(pool_alone, 1)
                    if b.off >= 2:
                        pool.wait_ge(ring2.sem_free(("y", 1)), ring2.reads(("y", 1), b.shifted(-2)))
                        pool.sem_inc(pool_alone, 1)
                    add_row(x1b[:, b.parity, :, :], x1[:], bo_c, x1b_ready)

            def scale_q(t, b):
                pool.wait_ge(qrec_ready, b.count(T, t + 1))
                pool.sem_inc(pool_alone, 1)
                w = qw[:, t % 2, :].rearrange("p (h d) -> p h d", d=DH)
                nc.gpsimd.tensor_tensor(w, w, qrec[:, t % 2, :].unsqueeze(2).broadcast_to([P, HID // DH, DH]), ALU.mult)\
                    .then_inc(qn_ready, 1)

            def split_max(g, b):
                pool.wait_ge(max_ring(b).sem_free(("m", g)), max_ring(b).reads(("m", g), b))
                pool.sem_inc(pool_alone, 1)
                nc.gpsimd.tensor_scalar(mpart[:, g % 2, 1, :], mrest[:, g % 2, :], 1.0, None, ALU.mult).then_inc(mmid_ready, 1)
                pool.wait_ge(mmid_ready, b.count(GR, g + 1))
                pool.sem_inc(pool_alone, 1)
                nc.gpsimd.tensor_tensor(mpart[:, g % 2, 2, :], mrest[:, g % 2, :], mpart[:, g % 2, 1, :], ALU.subtract)\
                    .then_inc(mlo_ready, 1)

            def stage2(name, b):
                if name == ("y", 1):
                    rsqrt(mv2, sd2, rs2, mean2, sd2_ready, rs2_ready, b, 2, 1)
                if name == ("f4", 1):
                    rsqrt(mv2, sd2, rs2, mean2, sd2_ready, rs2_ready, b, 2, 2)
                if name == ("x2T", 1):
                    for c in range(C):
                        pool.wait_ge(two_ring(b).sem_full(("x2T", c)), two_ring(b).fills(("x2T", c), b))
                        pool.sem_inc(pool_alone, 1)
                    pool.wait_ge(x2_ready, b.count(2 * T, T))
                    pool.sem_inc(pool_alone, 1)
                    add_row(x2[:], x2[:], b2_s, resid2_ready)

            def slot(s, bx, b1_, b2_):
                ones = stage1_pieces(s, b1_)
                um = s - MAX_LAG
                if bx is not None and um % 4 == 0 and 4 <= um <= UNITS:
                    split_max(um // 4 - 1, bx)
                for name in ones:
                    stage1(name, b1_)
                    if name in q_sum_at(b1_):
                        scale_q(q_sum_at(b1_)[name], b1_)
                for name in STAGE2_AT.get(s, []) if b2_ is not None else []:
                    stage2(name, b2_)

            run(pool, slot)


_INS = ["x", "ctx_768", "L0_attn_Wq", "L0_attn_Wk", "L0_attn_Wv", "L0_attn_Wo", "L0_attn_bo", "L0_xattn_Wq", "L0_xattn_Wk",
        "L0_xattn_Wv", "L0_xattn_Wo", "L0_xattn_bo", "L0_ffn_U1", "L0_ffn_V1", "L0_ffn_b1", "L0_ffn_U2", "L0_ffn_V2", "L0_ffn_b2"]


def kernel(**inputs):
    import numpy as np
    import concourse.bacc as bacc
    from concourse.bass_utils import run_bass_kernel_spmd

    nc = bacc.Bacc("TRN2", target_bir_lowering=False, num_devices=1)
    arrays, args = {}, []
    for name in _INS:
        a = np.ascontiguousarray(inputs[name])
        arrays[f"in_{name}"] = a
        args.append(nc.dram_tensor(f"in_{name}", a.shape, mybir.dt.from_np(a.dtype), kind="ExternalInput").ap())
    out = nc.dram_tensor("out_0", inputs["x"].shape, F32, kind="ExternalOutput").ap()
    decoder_layer(nc, *args, out)
    r = run_bass_kernel_spmd(nc, [arrays], core_ids=[0])
    return r.results[0]["out_0"]
```
